# Optimizing a Trainium2 kernel written in Bass

```python
import numpy as np
import jax
import jax.numpy as jnp

def _softmax(x, axis=-1):
    return jax.nn.softmax(x, axis=axis)

def _gelu(x):
    return jax.nn.gelu(x, approximate=True)

def _silu(x):
    return jax.nn.silu(x)

def _sigmoid(x):
    return jax.nn.sigmoid(x)

def _layernorm(x, axis=-1, eps=1e-05):
    m = jnp.mean(x, axis=axis, keepdims=True)
    v = jnp.var(x, axis=axis, keepdims=True)
    return (x - m) / jnp.sqrt(v + eps)

def _scatter_add(tgt, idx, src, axis=0):
    return tgt.at[idx].add(src)

def _segment_sum(src, seg, n):
    return jax.ops.segment_sum(src, seg, n)
kernel_name = 'mk_adj_preln_d2_adj_r2_ae43e3'

def setup_inputs(seed: int=0):
    np.random.seed(seed)
    _w = jnp.asarray

    def _rec_inputs():
        import jax
        import jax.numpy as jnp
        _gk = jax.random.key(seed)
        x = -0.0003929 + 0.9999 * jax.random.normal(jax.random.fold_in(_gk, 1), (32, 256, 256), jnp.float32)
        _a = jax.random.bernoulli(jax.random.fold_in(_gk, 2), 0.0625, (256, 256))
        _a = jnp.logical_or(_a, jnp.swapaxes(_a, -1, -2))
        _a = jnp.logical_or(_a, jnp.eye(256, dtype=bool))
        _af = _a.astype(jnp.float32)
        _af = _af * jax.random.uniform(jax.random.fold_in(_gk, 3), (256, 256), jnp.float32, 0.05, 1)
        adj = _af
        return (x, adj)
    x, adj = _rec_inputs()

    def _L0_gnn_setup():
        import jax, jax.numpy as jnp
        import numpy as np
        B, N, D, O = (8, 2048, 256, 256)
        key = jax.random.key(seed)
        k1, k2, k3, k4 = jax.random.split(key, 4)
        x = jax.random.normal(k1, (B, N, D), dtype=jnp.float32)
        adj = jax.random.uniform(k2, (N, N), dtype=jnp.float32)
        weight = jax.random.normal(k3, (D, O), dtype=jnp.float32) * 0.02
        bias = jax.random.normal(k4, (O,), dtype=jnp.float32) * 0.02
        return {'x': x, 'adj': adj, 'weight': weight, 'bias': bias}
    _L0_gnn_all = _L0_gnn_setup()
    _L0_gnn_in = {k: v for k, v in _L0_gnn_all.items() if k in ('weight', 'bias')}
    del _L0_gnn_all

    def _L1_gnn_setup():
        import jax, jax.numpy as jnp
        import numpy as np
        B, N, D, H = (4, 1024, 256, 8)
        HD = D // H
        key = jax.random.key(seed)
        ks = jax.random.split(key, 10)
        x = jax.random.normal(ks[0], (B, N, D), dtype=jnp.float32)
        adj = (jax.random.uniform(ks[1], (N, N)) < 0.1).astype(jnp.float32)
        s = 1.0 / np.sqrt(D)
        Wq = jax.random.normal(ks[2], (D, D), dtype=jnp.float32) * s
        Wk = jax.random.normal(ks[3], (D, D), dtype=jnp.float32) * s
        Wv = jax.random.normal(ks[4], (D, D), dtype=jnp.float32) * s
        Wo = jax.random.normal(ks[5], (D, D), dtype=jnp.float32) * s
        bq = jnp.zeros((D,), jnp.float32)
        bk = jnp.zeros((D,), jnp.float32)
        bv = jnp.zeros((D,), jnp.float32)
        bo = jnp.zeros((D,), jnp.float32)
        return {'x': x, 'adj': adj, 'Wq': Wq, 'bq': bq, 'Wk': Wk, 'bk': bk, 'Wv': Wv, 'bv': bv, 'Wo': Wo, 'bo': bo}
    _L1_gnn_all = _L1_gnn_setup()
    _L1_gnn_in = {k: v for k, v in _L1_gnn_all.items() if k in ('Wq', 'bq', 'Wk', 'bk', 'Wv', 'bv', 'Wo', 'bo')}
    del _L1_gnn_all
    return {'x': x, 'adj': adj, 'L0_gnn_weight': _L0_gnn_in['weight'], 'L0_gnn_bias': _L0_gnn_in['bias'], 'L1_gnn_Wq': _L1_gnn_in['Wq'], 'L1_gnn_bq': _L1_gnn_in['bq'], 'L1_gnn_Wk': _L1_gnn_in['Wk'], 'L1_gnn_bk': _L1_gnn_in['bk'], 'L1_gnn_Wv': _L1_gnn_in['Wv'], 'L1_gnn_bv': _L1_gnn_in['bv'], 'L1_gnn_Wo': _L1_gnn_in['Wo'], 'L1_gnn_bo': _L1_gnn_in['bo']}

def reference(x, adj, L0_gnn_weight, L0_gnn_bias, L1_gnn_Wq, L1_gnn_bq, L1_gnn_Wk, L1_gnn_bk, L1_gnn_Wv, L1_gnn_bv, L1_gnn_Wo, L1_gnn_bo):
    import jax
    import jax.numpy as jnp

    def _L0_gnn_ref(x, adj, weight, bias):
        import jax, jax.numpy as jnp
        import numpy as np
        B, N, D, O = (8, 2048, 256, 256)
        y = jnp.einsum('nm,bmd->bnd', adj, x)
        out = jnp.einsum('bnd,do->bno', y, weight) + bias
        return out

    def _L1_gnn_ref(x, adj, Wq, bq, Wk, bk, Wv, bv, Wo, bo):
        import jax, jax.numpy as jnp
        import numpy as np
        B, N, D, H = (4, 1024, 256, 8)
        HD = D // H
        b, n, d = x.shape
        q = (x @ Wq + bq).reshape(b, n, H, HD)
        k = (x @ Wk + bk).reshape(b, n, H, HD)
        v = (x @ Wv + bv).reshape(b, n, H, HD)
        scores = jnp.einsum('bqhd,bkhd->bhqk', q, k) / jnp.sqrt(jnp.float32(HD))
        scores = scores + (1.0 - adj)[None, None, :, :] * -1000000000.0
        attn = jax.nn.softmax(scores, axis=-1)
        out = jnp.einsum('bhqk,bkhd->bqhd', attn, v).reshape(b, n, d)
        return out @ Wo + bo
    h = jnp.maximum(_layernorm(x, axis=-1), 0.0)
    x = x + _L0_gnn_ref(h, adj, L0_gnn_weight, L0_gnn_bias)
    h = jnp.maximum(_layernorm(x, axis=-1), 0.0)
    x = x + _L1_gnn_ref(h, adj, L1_gnn_Wq, L1_gnn_bq, L1_gnn_Wk, L1_gnn_bk, L1_gnn_Wv, L1_gnn_bv, L1_gnn_Wo, L1_gnn_bo)
    return x

_drawn_inputs = setup_inputs


def setup_inputs(seed=0):
    import zlib

    import numpy as np

    out = dict(_drawn_inputs(seed))
    spreads = {'L1_gnn_bq': (0.0, 0.1),
     'L1_gnn_bk': (0.0, 0.1),
     'L1_gnn_bv': (0.0, 0.1),
     'L1_gnn_bo': (0.0, 0.1)}
    factors = {'L0_gnn_bias': 7.125}
    for name, (base, spread) in spreads.items():
        noise = np.random.default_rng([zlib.crc32(name.encode()), seed]).standard_normal(out[name].shape)
        drawn = base * np.exp(spread * noise) if base else spread * noise
        out[name] = jnp.asarray(drawn.astype(out[name].dtype))
    for name, factor in factors.items():
        out[name] = (out[name] * factor).astype(out[name].dtype)
    return out
```

```python
import math
from contextlib import ExitStack

import concourse.bass as bass
from concourse import mybir


class Batch:

    def __init__(self, i, u):
        self.i, self.u = i, u

    def plus(self, d):
        return Batch(self.i + (self.u + d) // 2, (self.u + d) % 2)

    @property
    def par(self):
        return self.u

    def index(self):
        return 2 * self.i + self.u

    def count(self, per, k):
        return self.i * (2 * per) + (self.u * per + k)

    def turn(self, per, k):
        return self.i * per + k


def wait(eng, sem, value):
    if isinstance(value, int) and value <= 0:
        return
    eng.wait_ge(sem, value)


def gnn_attention_kernel(nc, x, adj, w0, b0, wq, bq, wk, bk, wv, bv, wo, bo, out):
    f32, f32r = mybir.dt.float32, mybir.dt.float32r
    ALU = mybir.AluOpType
    ACT = mybir.ActivationFunctionType

    B, N, D = x.shape
    P = 128
    C = N // P
    K = D // P
    H = 8
    HD = D // H
    G = 2
    HG = H // G
    J = HG
    S_BANKS = 3
    LAST = B - 1
    SCALE = -1.0 / math.sqrt(HD)
    FAR = 1.0e9
    EPS = 1e-5
    BIG = 3.0e38

    with ExitStack() as ctx:
        def sb(name, shape, dt=f32):
            return ctx.enter_context(nc.sbuf_tensor(name, shape, dt))

        def sem(name):
            return ctx.enter_context(nc.semaphore(name))

        ident = sb("ident", [P, P])
        neghalf = sb("neghalf", [P, C])
        minus_one = sb("minus_one", [P, C])
        eps = sb("eps", [P, C])
        adj_nat = sb("adj_nat", [P, C, N])
        adj_t = sb("adj_t", [P, C, N])
        far = sb("far", [P, C, N])
        w0_sb = sb("w0_sb", [P, K, D])
        wq_sb = sb("wq_sb", [P, K, D])
        wk_sb = sb("wk_sb", [P, K, D])
        wv_sb = sb("wv_sb", [P, K, D])
        wo_sb = sb("wo_sb", [P, K, D])
        wqs = sb("wqs", [P, K, G, J * HD])
        wks = sb("wks", [P, K, G, J * HD])
        b0_bc = sb("b0_bc", [P, D])
        c_bc = sb("c_bc", [P, D])
        bo_bc = sb("bo_bc", [P, D])
        bv_col = sb("bv_col", [P, K])
        bq_col = sb("bq_col", [P, G])
        bqs = sb("bqs", [P, G])
        bk_col = sb("bk_col", [P, G])

        xt = sb("xt", [P, 2, C, D])
        xb = sb("xb", [P, 2, C, D])
        st0 = sb("st0", [P, C, 6])
        mv0 = sb("mv0", [P, C, 2])
        ve0 = sb("ve0", [P, 2, C])
        rs0 = sb("rs0", [P, C])
        nb0 = sb("nb0", [P, C])
        st1 = sb("st1", [P, C, 6])
        mv1 = sb("mv1", [P, C, 2])
        ve1 = sb("ve1", [P, 2, C])
        rs1 = sb("rs1", [P, C])
        nb1 = sb("nb1", [P, C])
        h0 = sb("h0", [P, C, D])
        yt = sb("yt", [P, K, N])
        x1 = sb("x1", [P, C, D])
        x1c = sb("x1c", [P, 2, C, D])
        h1 = sb("h1", [P, C, D])
        h1t = sb("h1t", [P, K, N])
        qk_src = sb("qk_src", [P, 2, 2, 2, G * N], f32r)
        qk_st = sb("qk_st", [P, 2, 2, J, G * N], f32r)
        v_sb = sb("v_sb", [P, 2, C, D])
        probs = sb("probs", [P, 4, C, N])
        nmax = sb("nmax", [P, 2, H, C])
        zsum = sb("zsum", [P, 2, H, C])
        zinv = sb("zinv", [P, 2, C, H, HD])
        probs_t = sb("probs_t", [P, H, C, N])
        zt = sb("zt", [P, G, N])
        attn_t = sb("attn_t", [P, G, N])
        x2 = sb("x2", [P, 2, C, D])

        s_ps = [ctx.enter_context(nc.psum_tensor(f"s_ps{n}", [P, C, N], f32)) for n in range(S_BANKS)]
        pt_ps = [ctx.enter_context(nc.psum_tensor(f"pt_ps{n}", [P, C, N], f32)) for n in range(2)]
        o_ps = ctx.enter_context(nc.psum_tensor("o_ps", [P, G, N], f32))
        d_ps = [ctx.enter_context(nc.psum_tensor(f"d_ps{n}", [P, 2, N], f32)) for n in range(2)]

        wait_carrier = sem("wait_carrier")
        const_in = sem("const_in")
        ident_zero, ident_ready = sem("ident_zero"), sem("ident_ready")
        adjt_mm, adjt_ready = sem("adjt_mm"), sem("adjt_ready")
        far_step, far_ready = sem("far_step"), sem("far_ready")
        wqk_ready, c_mm, c_ready = sem("wqk_ready"), sem("c_mm"), sem("c_ready")
        x_in = [sem("x_in0"), sem("x_in1")]
        st0_done, mv0_done, ve0_done, rs0_done, nb0_done = map(
            sem, ("st0_done", "mv0_done", "ve0_done", "rs0_done", "nb0_done"))
        xb_ready, h0_ready, yt_mm, yt_ready, out0_mm, x1_ready = map(
            sem, ("xb_ready", "h0_ready", "yt_mm", "yt_ready", "out0_mm", "x1_ready"))
        st1_done, mv1_done, ve1_done, rs1_done, nb1_done = map(
            sem, ("st1_done", "mv1_done", "ve1_done", "rs1_done", "nb1_done"))
        h1_ready, x1c_ready, h1t_mm, h1t_ready = map(sem, ("h1_ready", "x1c_ready", "h1t_mm", "h1t_ready"))
        q_mm, qhi_ready, qlo_ready = map(sem, ("q_mm", "qhi_ready", "qlo_ready"))
        k_mm, khi_ready, klo_ready = map(sem, ("k_mm", "khi_ready", "klo_ready"))
        v_mm, v_ready = sem("v_mm"), sem("v_ready")
        stacked = [[sem(f"stacked{p}_{j}") for j in range(J)] for p in range(2)]
        qk_mm, min_ready, exp_ready, pt_mm = map(sem, ("qk_mm", "min_ready", "exp_ready", "pt_mm"))
        pt_out = [sem("pt_out0"), sem("pt_out1")]
        pv_mm, zinv_ready, zt_mm, zt_ready = map(sem, ("pv_mm", "zinv_ready", "zt_mm", "zt_ready"))
        attn_ready, out1_mm, x2_ready = map(sem, ("attn_ready", "out1_mm", "x2_ready"))
        stored = [sem("stored0"), sem("stored1")]

        rows = lambda ap: ap.rearrange("(p c) d -> p c d", c=C)
        feat = lambda ap: ap.rearrange("(k p) n -> p k n", p=P)
        NCONST = 9 + 2 * J

        def steps(eng, step):
            for n in (-2, -1, 0, 1):
                step(Batch(n // 2, n % 2), n)
            with eng.Fori(1, B // 2 - 2) as i:
                for u in range(2):
                    step(Batch(i, u), None)
            for n in range(B - 4, B + 1):
                step(Batch(n // 2, n % 2), n)

        def has(n, d):
            return n is None or 0 <= n + d <= LAST

        def ahead(b, h):
            return (b, h, 0) if h < H else (b.plus(1), h - H, 1)

        block = ctx.enter_context(nc.Block())

        @block.sync
        def _(sp):
            def load(dst, src, short=False):
                sp.dma_start(dst, src, allow_slow_non_contiguous=short).then_inc(const_in, 16)

            def load_x(b):
                sp.dma_start(xt[:, b.par, :, :], rows(x[b.index(), :, :])).then_inc(x_in[b.par], 16)

            load(adj_nat[:, :, :], rows(adj))
            load_x(Batch(0, 0))
            load(w0_sb[:, :, :], feat(w0))
            load(b0_bc[:, :], b0.partition_broadcast(P))
            load(wq_sb[:, :, :], feat(wq))
            load(wk_sb[:, :, :], feat(wk))
            load(wv_sb[:, :, :], feat(wv))
            load(wo_sb[:, :, :], feat(wo))
            load(bo_bc[:, :], bo.partition_broadcast(P))
            load(bv_col[:, :], bv.rearrange("(k p) -> p k", p=P), short=True)
            for j in range(J):
                for col, src in ((bq_col, bq), (bk_col, bk)):
                    load(col[HD * j:HD * (j + 1), :],
                         src[2 * HD * j:2 * HD * (j + 1)].rearrange("(g d) -> d g", g=G), short=True)

            def step(b, n):
                if has(n, 3):
                    nxt = b.plus(3)
                    wait(sp, h0_ready, nxt.count(1, -1))
                    wait(sp, xb_ready, nxt.count(1, -1))
                    load_x(nxt)
                if has(n, -1):
                    prev = b.plus(-1)
                    wait(sp, x2_ready, prev.count(1, 1))
                    sp.dma_start(rows(out[prev.index(), :, :]), x2[:, prev.par, :, :]).then_inc(
                        stored[prev.par], 16)
                if has(n, 1):
                    nxt = b.plus(1)
                    p = nxt.par
                    wait(sp, qlo_ready, nxt.count(1, 1))
                    wait(sp, klo_ready, nxt.count(1, 1))
                    for j in range(J):
                        wait(sp, qk_mm, nxt.count(H, 2 * j + 2 - 2 * H))
                        for r in range(4):
                            src = qk_src[HD * j:HD * (j + 1), p, :, :, :].rearrange("p t s n -> p (t s) n")
                            first, second = r % 2, 2 + r // 2
                            sp.dma_start(
                                qk_st[HD * r:HD * (r + 1), p, :, j, :].bitcast(f32),
                                src[:, first:second + 1:second - first, :].bitcast(f32),
                            ).then_inc(stacked[p][j], 16)

            steps(sp, step)
            sp.wait_ge(stored[0], 16 * (B // 2))
            sp.wait_ge(stored[1], 16 * (B // 2))

        @block.gpsimd
        def _(pool):
            nc.gpsimd.memset(neghalf[:, :], -0.5)
            nc.gpsimd.memset(minus_one[:, :], -1.0)
            nc.gpsimd.memset(eps[:, :], EPS)
            nc.gpsimd.memset(ident[:, :], 0.0).then_inc(ident_zero, 1)
            pool.wait_ge(ident_zero, 1)
            nc.gpsimd.affine_select(out=ident[:, :], in_=ident[:, :], compare_op=ALU.not_equal, fill=1.0,
                                    base=0, pattern=[[-1, P]], channel_multiplier=1).then_inc(ident_ready, 1)
            pool.wait_ge(ident_ready, 1)
            pool.wait_ge(const_in, 16 * NCONST)
            pool.wait_ge(c_ready, 1)

            def norm_factors(b, mv, mv_done, ve, ve_done, rs, rs_done, nb, nb_done, used):
                wait(pool, mv_done, b.count(1, 1))
                nc.gpsimd.tensor_tensor(ve[:, 1, :], mv[:, :, 0], minus_one[:, :], ALU.mult)
                nc.gpsimd.tensor_tensor(ve[:, 0, :], mv[:, :, 1], eps[:, :], ALU.add).then_inc(ve_done, 1)
                wait(pool, used, b.count(1, 0))
                wait(pool, ve_done, b.count(1, 1))
                nc.gpsimd.tensor_tensor(rs[:, :], ve[:, 0, :], neghalf[:, :], ALU.pow).then_inc(rs_done, 1)
                wait(pool, rs_done, b.count(1, 1))
                nc.gpsimd.tensor_tensor(nb[:, :], ve[:, 1, :], rs[:, :], ALU.mult).then_inc(nb_done, 1)

            def step(b, n):
                if has(n, 1):
                    nxt = b.plus(1)
                    wait(pool, x1_ready, nxt.count(1, 1))
                    wait(pool, x2_ready, nxt.count(1, -1))
                    bc = c_bc[:, :].unsqueeze(1).broadcast_to([P, C, D])
                    nc.gpsimd.tensor_tensor(x1c[:, nxt.par, :, :], x1[:, :, :], bc,
                                            ALU.add).then_inc(x1c_ready, 1)
                if has(n, 2):
                    nxt = b.plus(2)
                    norm_factors(nxt, mv0, mv0_done, ve0, ve0_done, rs0, rs0_done, nb0, nb0_done, h0_ready)
                    wait(pool, x_in[nxt.par], nxt.turn(16, 16))
                    wait(pool, x1_ready, nxt.count(1, -1))
                    bc = b0_bc[:, :].unsqueeze(1).broadcast_to([P, C, D])
                    nc.gpsimd.tensor_tensor(xb[:, nxt.par, :, :], xt[:, nxt.par, :, :], bc,
                                            ALU.add).then_inc(xb_ready, 1)
                    norm_factors(nxt, mv1, mv1_done, ve1, ve1_done, rs1, rs1_done, nb1, nb1_done, h1_ready)

            steps(pool, step)

        @block.vector
        def _(dve):
            dve.wait_ge(const_in, 16 * NCONST)
            dve.wait_ge(adjt_mm, 1)
            nc.vector.tensor_copy(adj_t[:, :, :], pt_ps[0][:, :, :]).then_inc(adjt_ready, 1)
            by_chunk = adj_nat[:, :, :].rearrange("p c (k d) -> p c d k", d=C)
            for c in range(C):
                nc.vector.tensor_scalar(far[:, c, :].rearrange("p (d k) -> p d k", d=C), by_chunk[:, c, :, :],
                                        -1.0, 1.0, ALU.mult, ALU.add).then_inc(far_step, 1)
            dve.wait_ge(far_step, C)
            nc.vector.tensor_scalar(far[:, :, :], far[:, :, :], FAR, None, ALU.mult).then_inc(far_ready, 1)
            dve.wait_ge(far_ready, 1)
            for k in range(K):
                for dst, src, s in ((wqs, wq_sb, SCALE), (wks, wk_sb, 1.0)):
                    nc.vector.tensor_scalar(dst[:, k, :, :].rearrange("p g (j d) -> p g j d", j=J),
                                            src[:, k, :].rearrange("p (j g d) -> p g j d", j=J, g=G),
                                            s, None, ALU.mult)
            nc.vector.tensor_scalar(bqs[:, :], bq_col[:, :], SCALE, None, ALU.mult).then_inc(wqk_ready, 1)
            dve.wait_ge(wqk_ready, 1)
            dve.wait_ge(c_mm, 1)
            nc.vector.tensor_tensor(c_bc[:, :], pt_ps[1][:, 0, :], bo_bc[:, :], ALU.add).then_inc(c_ready, 1)

            def low_part(b, t, bank, col, hi_ready, lo_ready):
                wait(dve, hi_ready, b.count(1, 1))
                for g in range(G):
                    last = nc.vector.scalar_tensor_tensor(
                        out=qk_src[:, b.par, t, 1, N * g:N * (g + 1)], in0=bank[:, g, :],
                        scalar=col[:, g:g + 1], in1=qk_src[:, b.par, t, 0, N * g:N * (g + 1)].bitcast(f32),
                        op0=ALU.add, op1=ALU.subtract)
                last.then_inc(lo_ready, 1)

            def stats(b, src, st, st_done, mv, mv_done, used):
                for c in range(C):
                    last = nc.vector.bn_stats(st[:, c, :], src[:, c, :])
                last.then_inc(st_done, 1)
                wait(dve, st_done, b.count(1, 1))
                wait(dve, used, b.count(1, 0))
                dve.sem_inc(wait_carrier)
                for c in range(C):
                    last = nc.vector.bn_aggr(mv[:, c, :], st[:, c, :])
                last.then_inc(mv_done, 1)

            def step(b, n):
                for h in range(H):
                    bb, hh, d = ahead(b, h + 2)
                    if has(n, d):
                        wait(dve, qk_mm, bb.count(H, hh + 1))
                        dve.sem_inc(wait_carrier)
                        bank = s_ps[hh % S_BANKS]
                        for c in range(C):
                            last = nc.vector.tensor_tensor_reduce(
                                bank[:, c, :], bank[:, c, :], far[:, c, :], 1.0, BIG, ALU.add, ALU.min,
                                nmax[:, bb.par, hh, c:c + 1])
                        last.then_inc(min_ready, 1)
                    if h == 0 and has(n, 2):
                        nxt = b.plus(2)
                        wait(dve, x_in[nxt.par], nxt.turn(16, 16))
                        stats(nxt, xt[:, nxt.par, :, :], st0, st0_done, mv0, mv0_done, nb0_done)
                    if h == 1 and has(n, -1):
                        prev = b.plus(-1)
                        wait(dve, zt_ready, prev.count(1, 1))
                        wait(dve, pv_mm, prev.count(G, G))
                        wait(dve, out1_mm, prev.count(1, 0))
                        nc.vector.tensor_tensor(attn_t[:, :, :], o_ps[:, :, :], zt[:, :, :],
                                                ALU.mult).then_inc(attn_ready, 1)
                    if h == 2 and has(n, -1):
                        prev = b.plus(-1)
                        wait(dve, out1_mm, prev.count(1, 1))
                        wait(dve, x1c_ready, prev.count(1, 1))
                        wait(dve, stored[prev.par], prev.turn(16, 0))
                        nc.vector.tensor_tensor(x2[:, prev.par, :, :], d_ps[1][:, :, :],
                                                x1c[:, prev.par, :, :], ALU.add).then_inc(x2_ready, 1)
                    if h == 3 and has(n, 1):
                        low_part(b.plus(1), 0, d_ps[1], bqs, qhi_ready, qlo_ready)
                    if h == 4 and has(n, 1):
                        low_part(b.plus(1), 1, d_ps[0], bk_col, khi_ready, klo_ready)
                    if h % 2 == 1 and has(n, 0):
                        wait(dve, pt_mm, b.count(H, h + 1))
                        wait(dve, pv_mm, b.count(G, h // HG + 1 - G))
                        nc.vector.tensor_copy(probs_t[:, h, :, :], pt_ps[1][:, :, :]).then_inc(pt_out[1], 1)
                    if h == 7:
                        if has(n, 0):
                            wait(dve, exp_ready, b.count(H, H))
                            wait(dve, zt_mm, b.count(1, -1))
                            for c in range(C):
                                last = nc.vector.reciprocal(
                                    zinv[:, b.par, c, :, :],
                                    zsum[:, b.par, :, c].unsqueeze(2).broadcast_to([P, H, HD]))
                            last.then_inc(zinv_ready, 1)
                        if has(n, 2):
                            nxt = b.plus(2)
                            wait(dve, out0_mm, nxt.count(1, 1))
                            wait(dve, xb_ready, nxt.count(1, 1))
                            wait(dve, x1c_ready, nxt.count(1, 0))
                            wait(dve, h1_ready, nxt.count(1, 0))
                            nc.vector.tensor_tensor(x1[:, :, :], d_ps[1][:, :, :], xb[:, nxt.par, :, :],
                                                    ALU.add).then_inc(x1_ready, 1)
                            wait(dve, x1_ready, nxt.count(1, 1))
                            stats(nxt, x1, st1, st1_done, mv1, mv1_done, nb1_done)

            steps(dve, step)

        @block.scalar
        def _(act):
            act.wait_ge(const_in, 16 * NCONST)
            act.wait_ge(wqk_ready, 1)

            def normed(b, dst, src, rs, nb, nb_done, used, ready):
                wait(act, nb_done, b.count(1, 1))
                wait(act, used, b.count(1, 0))
                for c in range(C):
                    last = nc.scalar.activation(dst[:, c, :], src[:, c, :], ACT.Relu, bias=nb[:, c:c + 1],
                                                scale=rs[:, c:c + 1])
                last.then_inc(ready, 1)

            def high_part(b, t, bank, col, mm, ready):
                wait(act, mm, b.count(1, 1))
                for j in range(J):
                    wait(act, stacked[b.par][j], b.turn(64, 0))
                for g in range(G):
                    last = nc.scalar.activation(qk_src[:, b.par, t, 0, N * g:N * (g + 1)], bank[:, g, :],
                                                ACT.Identity, bias=col[:, g:g + 1])
                last.then_inc(ready, 1)

            def step(b, n):
                for h in range(H):
                    bb, hh, d = ahead(b, h + 1)
                    if has(n, d):
                        wait(act, min_ready, bb.count(H, hh + 1))
                        wait(act, pt_mm, bb.count(H, hh + 1 - 4))
                        if hh == 0:
                            wait(act, zinv_ready, bb.count(1, -1))
                        for c in range(C):
                            last = nc.scalar.activation(
                                probs[:, hh % 4, c, :], s_ps[hh % S_BANKS][:, c, :], ACT.Exp,
                                bias=nmax[:, bb.par, hh, c:c + 1], scale=-1.0,
                                accum_out=zsum[:, bb.par, hh, c:c + 1])
                        last.then_inc(exp_ready, 1)
                    if h % 2 == 0 and has(n, 0):
                        wait(act, pt_mm, b.count(H, h + 1))
                        wait(act, pv_mm, b.count(G, h // HG + 1 - G))
                        nc.scalar.activation(probs_t[:, h, :, :], pt_ps[0][:, :, :], ACT.Copy).then_inc(
                            pt_out[0], 1)
                    if h == 0 and has(n, -1):
                        prev = b.plus(-1)
                        wait(act, zt_mm, prev.count(1, 1))
                        wait(act, attn_ready, prev.count(1, 0))
                        nc.scalar.activation(zt[:, :, :], d_ps[0][:, :, :], ACT.Copy).then_inc(zt_ready, 1)
                    if h == 0 and has(n, 1):
                        normed(b.plus(1), h1, x1, rs1, nb1, nb1_done, h1t_mm, h1_ready)
                    if h == 1 and has(n, 1):
                        nxt = b.plus(1)
                        wait(act, h1t_mm, nxt.count(1, 1))
                        wait(act, v_mm, nxt.count(1, 0))
                        nc.scalar.activation(h1t[:, :, :], d_ps[0][:, :, :], ACT.Copy).then_inc(h1t_ready, 1)
                    if h == 2 and has(n, 1):
                        high_part(b.plus(1), 0, d_ps[1], bqs, q_mm, qhi_ready)
                    if h == 3 and has(n, 1):
                        high_part(b.plus(1), 1, d_ps[0], bk_col, k_mm, khi_ready)
                    if h == 3 and has(n, 2):
                        nxt = b.plus(2)
                        normed(nxt, h0, xt[:, nxt.par, :, :], rs0, nb0, nb0_done, yt_mm, h0_ready)
                    if h == 4 and has(n, 1):
                        nxt = b.plus(1)
                        wait(act, v_mm, nxt.count(1, 1))
                        wait(act, pv_mm, nxt.count(G, -G))
                        nc.scalar.activation(v_sb[:, nxt.par, :, :], d_ps[1][:, :, :], ACT.Copy).then_inc(
                            v_ready, 1)
                    if h == 5 and has(n, 2):
                        nxt = b.plus(2)
                        wait(act, yt_mm, nxt.count(1, 1))
                        wait(act, out0_mm, nxt.count(1, 0))
                        nc.scalar.activation(yt[:, :, :], d_ps[0][:, :, :], ACT.Copy).then_inc(yt_ready, 1)

            steps(act, step)

        @block.tensor
        def _(pe):
            def product(dst, left, right, terms):
                for t in range(terms):
                    last = nc.tensor.matmul(dst, left(t), right(t), start=(t == 0), stop=(t == terms - 1))
                return last

            pe.wait_ge(ident_ready, 1)
            pe.wait_ge(const_in, 16 * NCONST)
            for d in range(C):
                for c in range(C):
                    last = nc.tensor.transpose(pt_ps[0][:, d, P * c:P * (c + 1)], adj_nat[:, c, d::C],
                                               ident[:, :])
            last.then_inc(adjt_mm, 1)
            product(pt_ps[1][:, 0, :], lambda k: bv_col[:, k:k + 1].broadcast_to([P, P]),
                    lambda k: wo_sb[:, k, :], K).then_inc(c_mm, 1)
            pe.wait_ge(adjt_ready, 1)
            pe.wait_ge(c_ready, 1)
            pe.wait_ge(wqk_ready, 1)

            def weighted(b, g):
                wait(pe, v_ready, b.count(1, 1))
                for half in range(2):
                    wait(pe, pt_out[half], b.count(HG, 2 * (g + 1)))
                if g == 0:
                    wait(pe, attn_ready, b.count(1, 0))
                for c in range(C):
                    for j in range(HG):
                        h = HG * g + j
                        last = nc.tensor.matmul(o_ps[HD * j:HD * (j + 1), g, :],
                                                v_sb[:, b.par, c, HD * h:HD * (h + 1)],
                                                probs_t[:, h, c, :], start=(c == 0), stop=(c == C - 1))
                last.then_inc(pv_mm, 1)

            def step(b, n):
                for h in range(H):
                    bb, hh, d = ahead(b, h + 2)
                    if has(n, d):
                        if hh % 2 == 0:
                            wait(pe, stacked[bb.par][hh // 2], bb.turn(64, 64))
                        wait(pe, exp_ready, bb.count(H, hh - 2 if hh >= S_BANKS else (-1, 0, -2)[hh]))
                        for c in range(C):
                            last = nc.tensor.matmul(
                                s_ps[hh % S_BANKS][:, c, :],
                                qk_st[:, bb.par, 0, hh // 2, N * (hh % 2) + P * c:N * (hh % 2) + P * (c + 1)],
                                qk_st[:, bb.par, 1, hh // 2, N * (hh % 2):N * (hh % 2 + 1)],
                                start=True, stop=True)
                        last.then_inc(qk_mm, 1)
                    if has(n, 0):
                        wait(pe, exp_ready, b.count(H, h + 1))
                        wait(pe, pt_out[h % 2], b.count(HG, h // 2))
                        for d in range(C):
                            for c in range(C):
                                last = nc.tensor.transpose(pt_ps[h % 2][:, d, P * c:P * (c + 1)],
                                                           probs[:, h % 4, c, P * d:P * (d + 1)], ident[:, :])
                        last.then_inc(pt_mm, 1)
                    if h == 0 and has(n, -1):
                        prev = b.plus(-1)
                        wait(pe, zinv_ready, prev.count(1, 1))
                        if has(n, 1):
                            wait(pe, yt_ready, prev.count(1, 3))
                        else:
                            wait(pe, klo_ready, B)
                            wait(pe, zt_ready, prev.count(1, 0))
                        for g in range(G):
                            for c in range(C):
                                last = nc.tensor.transpose(
                                    d_ps[0][:, g, P * c:P * (c + 1)],
                                    zinv[:, prev.par, c, HG * g:HG * (g + 1), :].rearrange("p h d -> p (h d)"),
                                    ident[:, :])
                        last.then_inc(zt_mm, 1)
                        weighted(prev, 1)
                    if h == 1 and has(n, -1):
                        prev = b.plus(-1)
                        wait(pe, attn_ready, prev.count(1, 1))
                        if has(n, 1):
                            wait(pe, x1_ready, prev.count(1, 3))
                        else:
                            wait(pe, v_ready, B)
                            wait(pe, x2_ready, prev.count(1, 0))
                        for c in range(C):
                            last = product(d_ps[1][:, c, :], lambda g: attn_t[:, g, P * c:P * (c + 1)],
                                           lambda g: wo_sb[:, g, :], G)
                        last.then_inc(out1_mm, 1)
                    if h == 1 and has(n, 1):
                        nxt = b.plus(1)
                        wait(pe, h1_ready, nxt.count(1, 1))
                        wait(pe, zt_ready, nxt.count(1, -1))
                        wait(pe, yt_ready, nxt.count(1, 1))
                        for k in range(K):
                            for c in range(C):
                                last = nc.tensor.transpose(d_ps[0][:, k, P * c:P * (c + 1)],
                                                           h1[:, c, P * k:P * (k + 1)], ident[:, :])
                        last.then_inc(h1t_mm, 1)
                    if h == 2 and has(n, 1):
                        nxt = b.plus(1)
                        wait(pe, h1t_ready, nxt.count(1, 1))
                        wait(pe, x2_ready, nxt.count(1, -1))
                        wait(pe, x1_ready, nxt.count(1, 1))
                        for g in range(G):
                            last = product(d_ps[1][:, g, :], lambda k: wqs[:, k, g, :],
                                           lambda k: h1t[:, k, :], K)
                        last.then_inc(q_mm, 1)
                    if h == 3 and has(n, 1):
                        nxt = b.plus(1)
                        for g in range(G):
                            last = product(d_ps[0][:, g, :], lambda k: wks[:, k, g, :],
                                           lambda k: h1t[:, k, :], K)
                        last.then_inc(k_mm, 1)
                    if h == 4 and has(n, 1):
                        nxt = b.plus(1)
                        wait(pe, qlo_ready, nxt.count(1, 1))
                        for c in range(C):
                            last = product(d_ps[1][:, c, :], lambda k: h1t[:, k, P * c:P * (c + 1)],
                                           lambda k: wv_sb[:, k, :], K)
                        last.then_inc(v_mm, 1)
                    if h == 4 and has(n, 0):
                        weighted(b, 0)
                    if h == 5 and has(n, 2):
                        nxt = b.plus(2)
                        wait(pe, h0_ready, nxt.count(1, 1))
                        wait(pe, klo_ready, nxt.count(1, 0))
                        for k in range(K):
                            last = product(d_ps[0][:, k, :], lambda c: h0[:, c, P * k:P * (k + 1)],
                                           lambda c: adj_t[:, c, :], C)
                        last.then_inc(yt_mm, 1)
                    if h == 6 and has(n, 2):
                        nxt = b.plus(2)
                        wait(pe, yt_ready, nxt.count(1, 1))
                        wait(pe, v_ready, nxt.count(1, 0))
                        for c in range(C):
                            last = product(d_ps[1][:, c, :], lambda k: yt[:, k, P * c:P * (c + 1)],
                                           lambda k: w0_sb[:, k, :], K)
                        last.then_inc(out0_mm, 1)

            steps(pe, step)


_INS = ['x', 'adj', 'L0_gnn_weight', 'L0_gnn_bias', 'L1_gnn_Wq', 'L1_gnn_bq', 'L1_gnn_Wk', 'L1_gnn_bk',
        'L1_gnn_Wv', 'L1_gnn_bv', 'L1_gnn_Wo', 'L1_gnn_bo']


def kernel(**inputs):
    import numpy as _np
    import concourse.bacc as _bacc
    from concourse import mybir as _mybir
    from concourse.bass_utils import run_bass_kernel_spmd as _run

    nc = _bacc.Bacc("TRN2", target_bir_lowering=False, num_devices=1)
    arrays, args = {}, []
    for name in _INS:
        a = _np.ascontiguousarray(inputs[name])
        arrays[f"in_{name}_dram"] = a
        args.append(nc.dram_tensor(f"in_{name}_dram", a.shape, _mybir.dt.from_np(a.dtype), kind="ExternalInput").ap())
    args.append(nc.dram_tensor("out_0_dram", inputs["x"].shape, _mybir.dt.float32, kind="ExternalOutput").ap())
    gnn_attention_kernel(nc, *args)
    r = _run(nc, [arrays], core_ids=[0])
    return r.results[0]["out_0_dram"]
```

```python
import math
from contextlib import ExitStack

import concourse.bass as bass
from concourse import mybir


UNROLL = 4


class Batch:

    def __init__(self, i, u):
        self.i, self.u = i, u

    def plus(self, d):
        return Batch(self.i, self.u + d)

    def slot(self, ring):
        return self.u % ring

    def index(self):
        return self.i * UNROLL + self.u

    def count(self, per, k):
        return self.i * (UNROLL * per) + (self.u * per + k)

    def turn(self, per, k):
        return self.i * (UNROLL // 2 * per) + (self.u // 2 * per + k)


def wait(eng, sem, value):
    if isinstance(value, int) and value <= 0:
        return
    eng.wait_ge(sem, value)


def gnn_attention_kernel(nc, x, adj, w0, b0, wq, bq, wk, bk, wv, bv, wo, bo, out):
    f32, f32r = mybir.dt.float32, mybir.dt.float32r
    ALU = mybir.AluOpType
    ACT = mybir.ActivationFunctionType

    B, N, D = x.shape
    P = 128
    C = N // P
    K = D // P
    H = 8
    HD = D // H
    G = 2
    HG = H // G
    J = HG
    S_BANKS = 3
    LAST = B - 1
    SCALE = -1.0 / math.sqrt(HD)
    FAR = 1.0e9
    EPS = 1e-5
    BIG = 3.0e38
    HI, LO = 0, 1

    with ExitStack() as ctx:
        def sb(name, shape, dt=f32):
            return ctx.enter_context(nc.sbuf_tensor(name, shape, dt))

        def sem(name):
            return ctx.enter_context(nc.semaphore(name))

        ident = sb("ident", [P, P])
        neghalf = sb("neghalf", [P, C])
        minus_one = sb("minus_one", [P, C])
        eps = sb("eps", [P, C])
        ones = sb("ones", [P, 1])
        adj_nat = sb("adj_nat", [P, C, N])
        adj_f = sb("adj_f", [P, C, N])
        far = sb("far", [P, C, N])
        w_in = sb("w_in", [P, 5, K, D])
        wp = sb("wp", [P, 2, K, G, J * HD])
        adj_t = sb("adj_t", [P, 2, C, N], f32r)
        w0_s = sb("w0_s", [P, 2, K, D], f32r)
        wq_s = sb("wq_s", [P, 2, K, D], f32r)
        wk_s = sb("wk_s", [P, 2, K, D], f32r)
        wv_s = sb("wv_s", [P, 2, K, D], f32r)
        wo_s = sb("wo_s", [P, 2, K, D], f32r)
        b0_bc = sb("b0_bc", [P, D])
        c_bc = sb("c_bc", [P, D])
        bo_bc = sb("bo_bc", [P, D])
        bv_col = sb("bv_col", [P, K])
        bq_col = sb("bq_col", [P, G])
        bqs = sb("bqs", [P, G])
        bk_col = sb("bk_col", [P, G])

        xt = sb("xt", [P, 2, C, D])
        xb = sb("xb", [P, 2, C, D])
        st = [sb(f"st{n}", [P, C, 6]) for n in range(2)]
        mv = [sb(f"mv{n}", [P, C, 2]) for n in range(2)]
        ve = [sb(f"ve{n}", [P, 2, C]) for n in range(2)]
        rs = [sb(f"rs{n}", [P, C]) for n in range(2)]
        nb = [sb(f"nb{n}", [P, C]) for n in range(2)]
        h0 = sb("h0", [P, C, D])
        h0_s = sb("h0_s", [P, 2, C, D], f32r)
        yt = sb("yt", [P, K, N])
        yt_s = sb("yt_s", [P, 2, K, N], f32r)
        x1 = sb("x1", [P, C, D])
        x1c = sb("x1c", [P, 4, C, D])
        h1 = sb("h1", [P, C, D])
        h1t = sb("h1t", [P, K, N])
        h1t_s = sb("h1t_s", [P, 2, K, N], f32r)
        qk_f = sb("qk_f", [P, 2, G * N])
        qk_s = sb("qk_s", [P, 2, 2, 2, G * N], f32r)
        qk_st = sb("qk_st", [P, 2, 2, J, G * N], f32r)
        v_sb = sb("v_sb", [P, 4, C, D])
        probs = sb("probs", [P, 4, C, N])
        nmax = sb("nmax", [P, 2, H, C])
        zsum = sb("zsum", [P, 2, H, C])
        zinv = sb("zinv", [P, C, H])
        zrep = sb("zrep", [P, C, H, HD])
        probs_t = sb("probs_t", [P, H, C, N])
        zt = sb("zt", [P, G, N])
        attn = sb("attn", [P, G, N])
        attn_s = sb("attn_s", [P, 2, G, N], f32r)
        x2 = sb("x2", [P, 2, C, D])

        s_ps = [ctx.enter_context(nc.psum_tensor(f"s_ps{n}", [P, C, N], f32)) for n in range(S_BANKS)]
        pt_ps = [ctx.enter_context(nc.psum_tensor(f"pt_ps{n}", [P, C, N], f32)) for n in range(2)]
        o_ps = ctx.enter_context(nc.psum_tensor("o_ps", [P, G, N], f32))
        d_ps = [ctx.enter_context(nc.psum_tensor(f"d_ps{n}", [P, 2, N], f32)) for n in range(2)]

        wait_carrier = sem("wait_carrier")
        adj_in, graph_in, attn_in = sem("adj_in"), sem("graph_in"), sem("attn_in")
        ident_zero, ident_ready = sem("ident_zero"), sem("ident_ready")
        adjt_mm, adjt_full, adjt_hi, adjt_ready = map(sem, ("adjt_mm", "adjt_full", "adjt_hi", "adjt_ready"))
        w0_hi, w0_ready, far_step, far_ready = map(sem, ("w0_hi", "w0_ready", "far_step", "far_ready"))
        wp_ready, w_hi, w_ready, c_mm, c_ready = map(sem, ("wp_ready", "w_hi", "w_ready", "c_mm", "c_ready"))
        x_in = [sem("x_in0"), sem("x_in1")]
        st_done = [sem("st0_done"), sem("st1_done")]
        mv_done = [sem("mv0_done"), sem("mv1_done")]
        ve_done = [sem("ve0_done"), sem("ve1_done")]
        rs_done = [sem("rs0_done"), sem("rs1_done")]
        nb_done = [sem("nb0_done"), sem("nb1_done")]
        xb_ready, h0_f, h0_hi, h0_lo = map(sem, ("xb_ready", "h0_f", "h0_hi", "h0_lo"))
        yt_mm, yt_f, yt_hi, yt_lo = map(sem, ("yt_mm", "yt_f", "yt_hi", "yt_lo"))
        out0_mm, x1_ready = sem("out0_mm"), sem("x1_ready")
        h1_ready, x1c_ready = sem("h1_ready"), sem("x1c_ready")
        h1t_mm, h1t_f, h1t_hi, h1t_lo = map(sem, ("h1t_mm", "h1t_f", "h1t_hi", "h1t_lo"))
        qk_proj = [sem("q_proj"), sem("k_proj")]
        qk_full = [sem("q_full"), sem("k_full")]
        qk_hi = [sem("q_hi"), sem("k_hi")]
        qk_lo = [sem("q_lo"), sem("k_lo")]
        v_mm, v_ready = sem("v_mm"), sem("v_ready")
        stacked = [[sem(f"stacked{p}_{j}") for j in range(J)] for p in range(2)]
        qk_mm, min_ready, exp_ready, pt_mm = map(sem, ("qk_mm", "min_ready", "exp_ready", "pt_mm"))
        pt_out = [sem("pt_out0"), sem("pt_out1")]
        pv_mm, zinv_ready, zrep_ready, zt_mm, zt_ready = map(
            sem, ("pv_mm", "zinv_ready", "zrep_ready", "zt_mm", "zt_ready"))
        attn_f, attn_hi, attn_lo = sem("attn_f"), sem("attn_hi"), sem("attn_lo")
        out1_mm, x2_ready = sem("out1_mm"), sem("x2_ready")
        stored = [sem("stored0"), sem("stored1")]

        rows = lambda ap: ap.rearrange("(p c) d -> p c d", c=C)
        feat = lambda ap: ap.rearrange("(k p) n -> p k n", p=P)
        ATTN_LOADS = 6 + 2 * J

        FIRST_STEP = -4
        LOOP_FROM = 3
        LOOP_STEPS = (LAST - 5 - LOOP_FROM + 1) // UNROLL * UNROLL

        def steps(eng, step, setup=None):
            for n in range(FIRST_STEP, LOOP_FROM):
                step(Batch(0, n), n)
                if n == FIRST_STEP and setup:
                    setup()
            with eng.Fori(0, LOOP_STEPS // UNROLL) as i:
                for u in range(UNROLL):
                    step(Batch(i, LOOP_FROM + u), None)
            for n in range(LOOP_FROM + LOOP_STEPS, B + 1):
                step(Batch(0, n), n)

        def has(n, d):
            return n is None or 0 <= n + d <= LAST

        def ahead(b, h):
            return (b, h, 0) if h < H else (b.plus(1), h - H, 1)

        block = ctx.enter_context(nc.Block())

        @block.sync
        def _(sp):
            def load(dst, src, arrived, short=False):
                sp.dma_start(dst, src, allow_slow_non_contiguous=short).then_inc(arrived, 16)

            def load_x(b):
                sp.dma_start(xt[:, b.slot(2), :, :], rows(x[b.index(), :, :])).then_inc(x_in[b.slot(2)], 16)

            load(adj_nat[:, :, :], rows(adj), adj_in)
            load_x(Batch(0, 0))
            load(w_in[:, 0, :, :], feat(w0), graph_in)
            load(b0_bc[:, :], b0.partition_broadcast(P), graph_in)
            for n, w in enumerate((wq, wk, wv, wo)):
                load(w_in[:, 1 + n, :, :], feat(w), attn_in)
            load(bo_bc[:, :], bo.partition_broadcast(P), attn_in)
            load(bv_col[:, :], bv.rearrange("(k p) -> p k", p=P), attn_in, short=True)
            for j in range(J):
                for col, src in ((bq_col, bq), (bk_col, bk)):
                    load(col[HD * j:HD * (j + 1), :],
                         src[2 * HD * j:2 * HD * (j + 1)].rearrange("(g d) -> d g", g=G), attn_in, short=True)

            def store(b):
                wait(sp, x2_ready, b.count(1, 1))
                sp.dma_start(rows(out[b.index(), :, :]), x2[:, b.slot(2), :, :]).then_inc(stored[b.slot(2)], 16)

            def step(b, n):
                if has(n, -2):
                    store(b.plus(-2))
                if has(n, 5):
                    nxt = b.plus(5)
                    wait(sp, h0_lo, nxt.count(1, -1))
                    load_x(nxt)
                if has(n, 2):
                    nxt = b.plus(2)
                    p = nxt.slot(2)
                    wait(sp, qk_lo[1], nxt.count(1, 1))
                    for j in range(J):
                        for r in range(4):
                            src = qk_s[HD * j:HD * (j + 1), p, :, :, :].rearrange("p t s n -> p (t s) n")
                            first, second = r % 2, 2 + r // 2
                            sp.dma_start(
                                qk_st[HD * r:HD * (r + 1), p, :, j, :].bitcast(f32),
                                src[:, first:second + 1:second - first, :].bitcast(f32),
                            ).then_inc(stacked[p][j], 16)

            steps(sp, step)
            store(Batch(0, LAST))
            sp.wait_ge(stored[0], 16 * (B // 2))
            sp.wait_ge(stored[1], 16 * (B // 2))

        @block.gpsimd
        def _(pool):
            nc.gpsimd.memset(neghalf[:, :], -0.5)
            nc.gpsimd.memset(minus_one[:, :], -1.0)
            nc.gpsimd.memset(eps[:, :], EPS)
            nc.gpsimd.memset(ones[:, :], 1.0)
            nc.gpsimd.memset(ident[:, :], 0.0).then_inc(ident_zero, 1)
            pool.wait_ge(ident_zero, 1)
            nc.gpsimd.affine_select(out=ident[:, :], in_=ident[:, :], compare_op=ALU.not_equal, fill=1.0,
                                    base=0, pattern=[[-1, P]], channel_multiplier=1).then_inc(ident_ready, 1)
            pool.wait_ge(ident_ready, 1)

            def rest(dst, full, hi, done):
                nc.gpsimd.tensor_tensor(dst, full, hi.bitcast(f32), ALU.subtract).then_inc(done, 1)

            pool.wait_ge(adjt_hi, 1)
            rest(adj_t[:, LO], adj_f[:, :, :], adj_t[:, HI], adjt_ready)
            pool.wait_ge(w0_hi, 1)
            rest(w0_s[:, LO], w_in[:, 0], w0_s[:, HI], w0_ready)

            def setup():
                for m, (w, full) in enumerate(((wq_s, wp[:, 0].rearrange("p k g n -> p k (g n)")),
                                               (wk_s, wp[:, 1].rearrange("p k g n -> p k (g n)")),
                                               (wv_s, w_in[:, 3]), (wo_s, w_in[:, 4]))):
                    pool.wait_ge(w_hi, m + 1)
                    rest(w[:, LO], full, w[:, HI], w_ready)

            def factors(b, m, used):
                wait(pool, mv_done[m], b.count(1, 1))
                nc.gpsimd.tensor_tensor(ve[m][:, 1, :], mv[m][:, :, 0], minus_one[:, :], ALU.mult)
                nc.gpsimd.tensor_tensor(ve[m][:, 0, :], mv[m][:, :, 1], eps[:, :], ALU.add).then_inc(
                    ve_done[m], 1)
                wait(pool, used, b.count(1, 0))
                wait(pool, ve_done[m], b.count(1, 1))
                nc.gpsimd.tensor_tensor(rs[m][:, :], ve[m][:, 0, :], neghalf[:, :], ALU.pow).then_inc(
                    rs_done[m], 1)
                wait(pool, rs_done[m], b.count(1, 1))
                nc.gpsimd.tensor_tensor(nb[m][:, :], ve[m][:, 1, :], rs[m][:, :], ALU.mult).then_inc(
                    nb_done[m], 1)

            def low_part(b, split, full, f_ready, hi_ready, used, done):
                wait(pool, f_ready, b.count(1, 1))
                wait(pool, hi_ready, b.count(1, 1))
                wait(pool, used, b.count(1, 0))
                rest(split[:, LO], full[:, :, :], split[:, HI], done)

            def qk_low_part(b, t):
                wait(pool, qk_hi[t], b.count(1, 1))
                r = b.slot(2)
                rest(qk_s[:, r, t, LO, :], qk_f[:, t, :], qk_s[:, r, t, HI, :], qk_lo[t])

            def step(b, n):
                if has(n, -1):
                    prev = b.plus(-1)
                    wait(pool, zinv_ready, prev.count(1, 1))
                    wait(pool, zt_mm, prev.count(1, 0))
                    nc.gpsimd.tensor_tensor(
                        zrep[:, :, :, :].rearrange("p c h d -> p (c h) d"),
                        zinv[:, :, :].rearrange("p c h -> p (c h)").unsqueeze(2).broadcast_to([P, C * H, HD]),
                        ones[:, :].unsqueeze(1).broadcast_to([P, C * H, HD]), ALU.mult).then_inc(zrep_ready, 1)
                if has(n, 2):
                    nxt = b.plus(2)
                    if n == -2:
                        pool.wait_ge(c_ready, 1)
                    wait(pool, x1_ready, nxt.count(1, 1))
                    wait(pool, x2_ready, b.count(1, -1))
                    bc = c_bc[:, :].unsqueeze(1).broadcast_to([P, C, D])
                    nc.gpsimd.tensor_tensor(x1c[:, nxt.slot(4), :, :], x1[:, :, :], bc,
                                            ALU.add).then_inc(x1c_ready, 1)
                    low_part(nxt, h1t_s, h1t, h1t_f, h1t_hi, v_mm, h1t_lo)
                if has(n, 3):
                    low_part(b.plus(3), yt_s, yt, yt_f, yt_hi, out0_mm, yt_lo)
                if has(n, 4):
                    nxt = b.plus(4)
                    factors(nxt, 0, h0_f)
                    if n == FIRST_STEP:
                        pool.wait_ge(graph_in, 32)
                    wait(pool, x_in[nxt.slot(2)], nxt.turn(16, 16))
                    wait(pool, x1_ready, nxt.count(1, -1))
                    bc = b0_bc[:, :].unsqueeze(1).broadcast_to([P, C, D])
                    nc.gpsimd.tensor_tensor(xb[:, nxt.slot(2), :, :], xt[:, nxt.slot(2), :, :], bc,
                                            ALU.add).then_inc(xb_ready, 1)
                if has(n, -1):
                    low_part(b.plus(-1), attn_s, attn, attn_f, attn_hi, out1_mm, attn_lo)
                if has(n, 2):
                    qk_low_part(b.plus(2), 0)
                if has(n, 3):
                    factors(b.plus(3), 1, h1_ready)
                if has(n, 4):
                    low_part(b.plus(4), h0_s, h0, h0_f, h0_hi, yt_mm, h0_lo)
                if has(n, 2):
                    qk_low_part(b.plus(2), 1)

            steps(pool, step, setup)

        @block.vector
        def _(dve):
            dve.wait_ge(adjt_mm, 1)
            nc.vector.tensor_copy(adj_f[:, :, :], pt_ps[0][:, :, :]).then_inc(adjt_full, 1)
            dve.wait_ge(adjt_full, 1)
            nc.vector.tensor_copy(adj_t[:, HI], adj_f[:, :, :]).then_inc(adjt_hi, 1)
            dve.wait_ge(graph_in, 32)
            nc.vector.tensor_copy(w0_s[:, HI], w_in[:, 0]).then_inc(w0_hi, 1)

            def setup():
                dve.wait_ge(attn_in, 16 * ATTN_LOADS)
                for k in range(K):
                    for m, s in ((0, SCALE), (1, 1.0)):
                        nc.vector.tensor_scalar(wp[:, m, k, :, :].rearrange("p g (j d) -> p g j d", j=J),
                                                w_in[:, 1 + m, k, :].rearrange("p (j g d) -> p g j d", j=J, g=G),
                                                s, None, ALU.mult)
                nc.vector.tensor_scalar(bqs[:, :], bq_col[:, :], SCALE, None, ALU.mult).then_inc(wp_ready, 1)
                dve.wait_ge(wp_ready, 1)
                for w, full in ((wq_s, wp[:, 0].rearrange("p k g n -> p k (g n)")),
                                (wk_s, wp[:, 1].rearrange("p k g n -> p k (g n)")),
                                (wv_s, w_in[:, 3]), (wo_s, w_in[:, 4])):
                    nc.vector.tensor_copy(w[:, HI], full).then_inc(w_hi, 1)
                by_chunk = adj_nat[:, :, :].rearrange("p c (k d) -> p c d k", d=C)
                for c in range(C):
                    nc.vector.tensor_scalar(far[:, c, :].rearrange("p (d k) -> p d k", d=C),
                                            by_chunk[:, c, :, :], -1.0, 1.0, ALU.mult,
                                            ALU.add).then_inc(far_step, 1)
                dve.wait_ge(far_step, C)
                nc.vector.tensor_scalar(far[:, :, :], far[:, :, :], FAR, None, ALU.mult).then_inc(far_ready, 1)
                dve.wait_ge(far_ready, 1)
                dve.wait_ge(c_mm, 1)
                nc.vector.tensor_tensor(c_bc[:, :], pt_ps[1][:, 0, :], bo_bc[:, :], ALU.add).then_inc(c_ready, 1)

            def high_part(b, split, full, f_ready, used, done):
                wait(dve, f_ready, b.count(1, 1))
                wait(dve, used, b.count(1, 0))
                nc.vector.tensor_copy(split[:, HI], full[:, :, :]).then_inc(done, 1)

            def qk_high_part(b, t):
                r = b.slot(2)
                wait(dve, qk_full[t], b.count(1, 1))
                for j in range(J):
                    wait(dve, stacked[r][j], b.turn(64, 0))
                nc.vector.tensor_copy(qk_s[:, r, t, HI, :], qk_f[:, t, :]).then_inc(qk_hi[t], 1)

            def stats(b, src, m):
                for c in range(C):
                    last = nc.vector.bn_stats(st[m][:, c, :], src[:, c, :])
                last.then_inc(st_done[m], 1)
                wait(dve, st_done[m], b.count(1, 1))
                wait(dve, nb_done[m], b.count(1, 0))
                dve.sem_inc(wait_carrier)
                for c in range(C):
                    last = nc.vector.bn_aggr(mv[m][:, c, :], st[m][:, c, :])
                last.then_inc(mv_done[m], 1)

            def move_probs(b, h):
                wait(dve, pt_mm, b.count(H, h + 1))
                wait(dve, pv_mm, b.count(G, h // HG + 1 - G))
                nc.vector.tensor_copy(probs_t[:, h, :, :], pt_ps[h % 2][:, :, :]).then_inc(pt_out[h % 2], 1)

            def step(b, n):
                for h in range(H):
                    if h in (2, 4) and has(n, 0):
                        move_probs(b, h - 1)
                    bb, hh, d = ahead(b, h + 2)
                    if has(n, d):
                        wait(dve, qk_mm, bb.count(H, hh + 1))
                        dve.sem_inc(wait_carrier)
                        bank = s_ps[hh % S_BANKS]
                        for c in range(C):
                            last = nc.vector.tensor_tensor_reduce(
                                bank[:, c, :], bank[:, c, :], far[:, c, :], 1.0, BIG, ALU.add, ALU.min,
                                nmax[:, bb.slot(2), hh, c:c + 1])
                        last.then_inc(min_ready, 1)
                    if h == 1 and has(n, 2):
                        high_part(b.plus(2), h1t_s, h1t, h1t_f, v_mm, h1t_hi)
                    if h == 2 and has(n, 3):
                        high_part(b.plus(3), yt_s, yt, yt_f, out0_mm, yt_hi)
                    if h == 2 and has(n, 4):
                        nxt = b.plus(4)
                        wait(dve, x_in[nxt.slot(2)], nxt.turn(16, 16))
                        stats(nxt, xt[:, nxt.slot(2), :, :], 0)
                    if h == 4 and has(n, -1):
                        prev = b.plus(-1)
                        wait(dve, zt_ready, prev.count(1, 1))
                        wait(dve, pv_mm, prev.count(G, G))
                        wait(dve, attn_lo, prev.count(1, 0))
                        nc.vector.tensor_tensor(attn[:, :, :], o_ps[:, :, :], zt[:, :, :],
                                                ALU.mult).then_inc(attn_f, 1)
                        high_part(prev, attn_s, attn, attn_f, out1_mm, attn_hi)
                    if h == 5 and has(n, 2):
                        qk_high_part(b.plus(2), 0)
                    if h == 5 and has(n, 3):
                        nxt = b.plus(3)
                        wait(dve, out0_mm, nxt.count(1, 1))
                        wait(dve, xb_ready, nxt.count(1, 1))
                        wait(dve, x1c_ready, nxt.count(1, 0))
                        wait(dve, h1_ready, nxt.count(1, 0))
                        nc.vector.tensor_tensor(x1[:, :, :], d_ps[0][:, :, :], xb[:, nxt.slot(2), :, :],
                                                ALU.add).then_inc(x1_ready, 1)
                        wait(dve, x1_ready, nxt.count(1, 1))
                        dve.sem_inc(wait_carrier)
                        stats(nxt, x1, 1)
                    if h == 6 and has(n, 0):
                        move_probs(b, 6)
                    if h == 6 and has(n, 4):
                        high_part(b.plus(4), h0_s, h0, h0_f, yt_mm, h0_hi)
                    if h == 7:
                        if has(n, 2):
                            qk_high_part(b.plus(2), 1)
                        if has(n, 0):
                            wait(dve, exp_ready, b.count(H, H))
                            wait(dve, zrep_ready, b.count(1, 0))
                            nc.vector.reciprocal(zinv[:, :, :], zsum[:, b.slot(2), :, :].rearrange("p h c -> p c h")).then_inc(
                                zinv_ready, 1)
                            move_probs(b, 7)
                        if has(n, -1):
                            prev = b.plus(-1)
                            wait(dve, out1_mm, prev.count(1, 1))
                            wait(dve, x1c_ready, prev.count(1, 1))
                            wait(dve, stored[prev.slot(2)], prev.turn(16, 0))
                            nc.vector.tensor_tensor(x2[:, prev.slot(2), :, :], d_ps[1][:, :, :],
                                                    x1c[:, prev.slot(4), :, :], ALU.add).then_inc(x2_ready, 1)

            steps(dve, step, setup)

        @block.scalar
        def _(act):
            def normed(b, dst, src, m, used, ready):
                wait(act, nb_done[m], b.count(1, 1))
                wait(act, used, b.count(1, 0))
                for c in range(C):
                    last = nc.scalar.activation(dst[:, c, :], src[:, c, :], ACT.Relu, bias=nb[m][:, c:c + 1],
                                                scale=rs[m][:, c:c + 1])
                last.then_inc(ready, 1)

            def move(b, dst, bank, filled, used, ready, ring=1):
                wait(act, filled, b.count(1, 1))
                wait(act, used, b.count(1, 1 - ring))
                nc.scalar.activation(dst, bank[:, :, :], ACT.Copy).then_inc(ready, 1)

            def qk_move(b, t, col):
                wait(act, qk_proj[t], b.count(1, 1))
                wait(act, qk_lo[t], b.count(1, 0))
                for g in range(G):
                    last = nc.scalar.activation(qk_f[:, t, N * g:N * (g + 1)], d_ps[1][:, g, :], ACT.Identity,
                                                bias=col[:, g:g + 1])
                last.then_inc(qk_full[t], 1)

            def move_probs(b, h):
                wait(act, pt_mm, b.count(H, h + 1))
                wait(act, pv_mm, b.count(G, h // HG + 1 - G))
                nc.scalar.activation(probs_t[:, h, :, :], pt_ps[h % 2][:, :, :], ACT.Copy).then_inc(
                    pt_out[h % 2], 1)

            def step(b, n):
                for h in range(H):
                    if h == 2 and has(n, 3):
                        move(b.plus(3), yt[:, :, :], d_ps[1], yt_mm, yt_lo, yt_f)
                    bb, hh, d = ahead(b, h + 1)
                    if has(n, d):
                        wait(act, min_ready, bb.count(H, hh + 1))
                        wait(act, pt_mm, bb.count(H, hh + 1 - 4))
                        if hh == 0:
                            wait(act, zinv_ready, bb.count(1, -1))
                        for c in range(C):
                            last = nc.scalar.activation(
                                probs[:, hh % 4, c, :], s_ps[hh % S_BANKS][:, c, :], ACT.Exp,
                                bias=nmax[:, bb.slot(2), hh, c:c + 1], scale=-1.0,
                                accum_out=zsum[:, bb.slot(2), hh, c:c + 1])
                        last.then_inc(exp_ready, 1)
                    if h in (3, 5) and has(n, 0):
                        move_probs(b, h - 1)
                    if h == 7 and has(n, 2):
                        nxt = b.plus(2)
                        move(nxt, v_sb[:, nxt.slot(4), :, :], d_ps[0], v_mm, x2_ready, v_ready, ring=4)
                    if h == 0 and has(n, 0):
                        move_probs(b, 0)
                    if h == 0 and has(n, 2):
                        move(b.plus(2), h1t[:, :, :], d_ps[0], h1t_mm, h1t_lo, h1t_f)
                    if h == 3 and has(n, -1):
                        move(b.plus(-1), zt[:, :, :], d_ps[0], zt_mm, attn_f, zt_ready)
                    if h == 4 and has(n, 2):
                        qk_move(b.plus(2), 0, bqs)
                    if h == 5 and has(n, 4):
                        nxt = b.plus(4)
                        normed(nxt, h0, xt[:, nxt.slot(2), :, :], 0, h0_lo, h0_f)
                    if h == 6 and has(n, 2):
                        qk_move(b.plus(2), 1, bk_col)
                    if h == 6 and has(n, 0):
                        move_probs(b, 5)
                    if h == 7 and has(n, 3):
                        normed(b.plus(3), h1, x1, 1, h1t_mm, h1_ready)

            steps(act, step)

        @block.tensor
        def _(pe):
            pe.wait_ge(ident_ready, 1)
            pe.wait_ge(adj_in, 16)
            for d in range(C):
                for c in range(C):
                    last = nc.tensor.transpose(pt_ps[0][:, d, P * c:P * (c + 1)], adj_nat[:, c, d::C],
                                               ident[:, :])
            last.then_inc(adjt_mm, 1)

            def setup():
                pe.wait_ge(attn_in, 16 * ATTN_LOADS)
                for k in range(K):
                    last = nc.tensor.matmul(pt_ps[1][:, 0, :], bv_col[:, k:k + 1].broadcast_to([P, P]),
                                            w_in[:, 4, k, :], start=(k == 0), stop=(k == K - 1))
                last.then_inc(c_mm, 1)

            def product(dst, left, right, chunks):
                passes = [(k, a, b) for a, b in ((LO, HI), (HI, LO), (HI, HI)) for k in range(chunks)]
                for m, (k, a, b) in enumerate(passes):
                    last = nc.tensor.matmul(dst, left(a, k), right(b, k), start=(m == 0),
                                            stop=(m == len(passes) - 1))
                return last

            def weighted(b, g):
                wait(pe, v_ready, b.count(1, 1))
                for half in range(2):
                    wait(pe, pt_out[half], b.count(HG, 2 * (g + 1)))
                if g == 0:
                    wait(pe, attn_f, b.count(1, 0))
                for c in range(C):
                    for j in range(HG):
                        h = HG * g + j
                        last = nc.tensor.matmul(o_ps[HD * j:HD * (j + 1), g, :],
                                                v_sb[:, b.slot(4), c, HD * h:HD * (h + 1)],
                                                probs_t[:, h, c, :], start=(c == 0), stop=(c == C - 1))
                last.then_inc(pv_mm, 1)

            def qk_project(b, t, w):
                for g in range(G):
                    last = product(d_ps[1][:, g, :], lambda s, k: w[:, s, k, P * g:P * (g + 1)],
                                   lambda s, k: h1t_s[:, s, k, :], K)
                last.then_inc(qk_proj[t], 1)

            def step(b, n):
                for h in range(H):
                    bb, hh, d = ahead(b, h + 2)
                    if has(n, d):
                        if hh % 2 == 0:
                            wait(pe, stacked[bb.slot(2)][hh // 2], bb.turn(64, 64))
                        wait(pe, exp_ready, bb.count(H, hh - 2 if hh >= S_BANKS else (-1, 0, -2)[hh]))
                        for c in range(C):
                            last = nc.tensor.matmul(
                                s_ps[hh % S_BANKS][:, c, :],
                                qk_st[:, bb.slot(2), 0, hh // 2,
                                      N * (hh % 2) + P * c:N * (hh % 2) + P * (c + 1)],
                                qk_st[:, bb.slot(2), 1, hh // 2, N * (hh % 2):N * (hh % 2 + 1)],
                                start=True, stop=True)
                        last.then_inc(qk_mm, 1)
                    if has(n, 0):
                        wait(pe, exp_ready, b.count(H, h + 1))
                        wait(pe, pt_out[h % 2], b.count(HG, h // 2))
                        for d in range(C):
                            for c in range(C):
                                last = nc.tensor.transpose(pt_ps[h % 2][:, d, P * c:P * (c + 1)],
                                                           probs[:, h % 4, c, P * d:P * (d + 1)], ident[:, :])
                        last.then_inc(pt_mm, 1)
                    if h == 0 and has(n, 2):
                        nxt = b.plus(2)
                        wait(pe, h1_ready, nxt.count(1, 1))
                        wait(pe, v_ready, b.count(1, 2))
                        for k in range(K):
                            for c in range(C):
                                last = nc.tensor.transpose(d_ps[0][:, k, P * c:P * (c + 1)],
                                                           h1[:, c, P * k:P * (k + 1)], ident[:, :])
                        last.then_inc(h1t_mm, 1)
                    if h == 1 and has(n, 3):
                        nxt = b.plus(3)
                        if n == -3:
                            pe.wait_ge(adjt_ready, 1)
                        wait(pe, h0_hi, nxt.count(1, 1))
                        wait(pe, h0_lo, nxt.count(1, 1))
                        if has(n, -2):
                            wait(pe, x2_ready, b.count(1, -1))
                        else:
                            wait(pe, qk_full[1], b.count(1, 2))
                            wait(pe, yt_f, b.count(1, 3))
                        for k in range(K):
                            last = product(d_ps[1][:, k, :], lambda s, c: h0_s[:, s, c, P * k:P * (k + 1)],
                                           lambda s, c: adj_t[:, s, c, :], C)
                        last.then_inc(yt_mm, 1)
                    if h == 2 and has(n, -1):
                        prev = b.plus(-1)
                        wait(pe, zrep_ready, prev.count(1, 1))
                        if has(n, 2):
                            wait(pe, h1t_f, b.count(1, 3))
                        elif has(n, 1):
                            wait(pe, v_ready, b.count(1, 2))
                        else:
                            wait(pe, zt_ready, prev.count(1, 0))
                        for g in range(G):
                            for c in range(C):
                                last = nc.tensor.transpose(
                                    d_ps[0][:, g, P * c:P * (c + 1)],
                                    zrep[:, c, HG * g:HG * (g + 1), :].rearrange("p h d -> p (h d)"),
                                    ident[:, :])
                        last.then_inc(zt_mm, 1)
                        weighted(prev, 1)
                    if h == 3 and has(n, 2):
                        nxt = b.plus(2)
                        if n == -2:
                            pe.wait_ge(w_ready, 4)
                        wait(pe, h1t_hi, nxt.count(1, 1))
                        wait(pe, h1t_lo, nxt.count(1, 1))
                        if has(n, 3):
                            wait(pe, yt_f, b.count(1, 4))
                        else:
                            wait(pe, x2_ready, b.count(1, -1))
                        qk_project(nxt, 0, wq_s)
                    if h == 4 and has(n, 3):
                        nxt = b.plus(3)
                        if n == -3:
                            pe.wait_ge(w0_ready, 1)
                        wait(pe, yt_hi, nxt.count(1, 1))
                        wait(pe, yt_lo, nxt.count(1, 1))
                        if has(n, -1):
                            wait(pe, zt_ready, b.count(1, 0))
                        else:
                            wait(pe, h1t_f, b.count(1, 3))
                        for c in range(C):
                            last = product(d_ps[0][:, c, :], lambda s, k: yt_s[:, s, k, P * c:P * (c + 1)],
                                           lambda s, k: w0_s[:, s, k, :], K)
                        last.then_inc(out0_mm, 1)
                    if h == 5 and has(n, 2):
                        nxt = b.plus(2)
                        wait(pe, qk_full[0], nxt.count(1, 1))
                        qk_project(nxt, 1, wk_s)
                    if h == 5 and has(n, 0):
                        weighted(b, 0)
                    if h == 6 and has(n, 2):
                        nxt = b.plus(2)
                        if has(n, 3):
                            wait(pe, x1_ready, b.count(1, 4))
                        else:
                            wait(pe, zt_ready, b.count(1, 0))
                        for c in range(C):
                            last = product(d_ps[0][:, c, :], lambda s, k: h1t_s[:, s, k, P * c:P * (c + 1)],
                                           lambda s, k: wv_s[:, s, k, :], K)
                        last.then_inc(v_mm, 1)
                    if h == 7 and has(n, -1):
                        prev = b.plus(-1)
                        wait(pe, attn_hi, prev.count(1, 1))
                        wait(pe, attn_lo, prev.count(1, 1))
                        if has(n, 2):
                            wait(pe, qk_full[1], b.count(1, 3))
                        else:
                            wait(pe, x2_ready, prev.count(1, 0))
                        for c in range(C):
                            last = product(d_ps[1][:, c, :], lambda s, g: attn_s[:, s, g, P * c:P * (c + 1)],
                                           lambda s, g: wo_s[:, s, g, :], G)
                        last.then_inc(out1_mm, 1)

            steps(pe, step, setup)


_INS = ['x', 'adj', 'L0_gnn_weight', 'L0_gnn_bias', 'L1_gnn_Wq', 'L1_gnn_bq', 'L1_gnn_Wk', 'L1_gnn_bk',
        'L1_gnn_Wv', 'L1_gnn_bv', 'L1_gnn_Wo', 'L1_gnn_bo']


def kernel(**inputs):
    import numpy as _np
    import concourse.bacc as _bacc
    from concourse import mybir as _mybir
    from concourse.bass_utils import run_bass_kernel_spmd as _run

    nc = _bacc.Bacc("TRN2", target_bir_lowering=False, num_devices=1)
    arrays, args = {}, []
    for name in _INS:
        a = _np.ascontiguousarray(inputs[name])
        arrays[f"in_{name}_dram"] = a
        args.append(nc.dram_tensor(f"in_{name}_dram", a.shape, _mybir.dt.from_np(a.dtype), kind="ExternalInput").ap())
    args.append(nc.dram_tensor("out_0_dram", inputs["x"].shape, _mybir.dt.float32, kind="ExternalOutput").ap())
    gnn_attention_kernel(nc, *args)
    r = _run(nc, [arrays], core_ids=[0])
    return r.results[0]["out_0_dram"]
```

```python
import math
from contextlib import ExitStack

import concourse.bass as bass
from concourse import mybir


UNROLL = 4


class Batch:

    def __init__(self, i, u):
        self.i, self.u = i, u

    def plus(self, d):
        return Batch(self.i, self.u + d)

    def slot(self, ring):
        return self.u % ring

    def index(self):
        return self.i * UNROLL + self.u

    def count(self, per, k):
        return self.i * (UNROLL * per) + (self.u * per + k)

    def turn(self, ring, per, k):
        return self.i * (UNROLL // ring * per) + (self.u // ring * per + k)


def wait(eng, sem, value):
    if isinstance(value, int) and value <= 0:
        return
    eng.wait_ge(sem, value)


def gnn_attention_kernel(nc, x, adj, w0, b0, wq, bq, wk, bk, wv, bv, wo, bo, out):
    f32, f32r = mybir.dt.float32, mybir.dt.float32r
    ALU = mybir.AluOpType
    ACT = mybir.ActivationFunctionType

    B, N, D = x.shape
    P = 128
    C = N // P
    K = D // P
    H = 8
    HD = D // H
    G = 2
    HG = H // G
    J = HG
    S_BANKS = 3
    LAST = B - 1
    SCALE = -1.0 / math.sqrt(HD)
    FAR = 1.0e9
    EPS = 1e-5
    BIG = 3.0e38
    HI, LO = 0, 1

    with ExitStack() as ctx:
        def sb(name, shape, dt=f32):
            return ctx.enter_context(nc.sbuf_tensor(name, shape, dt))

        def sem(name):
            return ctx.enter_context(nc.semaphore(name))

        ident = sb("ident", [P, P])
        neghalf = sb("neghalf", [P, C])
        minus_one = sb("minus_one", [P, C])
        eps = sb("eps", [P, C])
        ones = sb("ones", [P, 1])
        adj_nat = sb("adj_nat", [P, C, N])
        adj_f = sb("adj_f", [P, C, N])
        far = sb("far", [P, C, N])
        w_in = sb("w_in", [P, 5, K, D])
        wp = sb("wp", [P, 2, K, G, J * HD])
        adj_t = sb("adj_t", [P, 2, C, N], f32r)
        w0_s = sb("w0_s", [P, 2, K, D], f32r)
        wq_s = sb("wq_s", [P, 2, K, D], f32r)
        wk_s = sb("wk_s", [P, 2, K, D], f32r)
        wv_s = sb("wv_s", [P, 2, K, D], f32r)
        wo_s = sb("wo_s", [P, 2, K, D], f32r)
        b0_bc = sb("b0_bc", [P, D])
        c_bc = sb("c_bc", [P, D])
        bo_bc = sb("bo_bc", [P, D])
        bv_col = sb("bv_col", [P, K])
        bq_col = sb("bq_col", [P, G])
        bqs = sb("bqs", [P, G])
        bk_col = sb("bk_col", [P, G])

        xt = sb("xt", [P, 4, C, D])
        xb = sb("xb", [P, 2, C, D])
        st = [sb(f"st{n}", [P, C, 6]) for n in range(2)]
        mv = [sb(f"mv{n}", [P, C, 2]) for n in range(2)]
        ve = [sb(f"ve{n}", [P, 2, C]) for n in range(2)]
        rs = [sb(f"rs{n}", [P, C]) for n in range(2)]
        nb = [sb(f"nb{n}", [P, C]) for n in range(2)]
        h0 = sb("h0", [P, C, D])
        h0_s = sb("h0_s", [P, 2, C, D], f32r)
        yt = sb("yt", [P, K, N])
        yt_s = sb("yt_s", [P, 2, K, N], f32r)
        x1 = sb("x1", [P, C, D])
        x1c = sb("x1c", [P, 4, C, D])
        h1 = sb("h1", [P, C, D])
        h1t = sb("h1t", [P, K, N])
        h1t_s = sb("h1t_s", [P, 2, K, N], f32r)
        qk_f = sb("qk_f", [P, 2, G * N])
        qk_s = sb("qk_s", [P, 2, 2, 2, G * N], f32r)
        qk_st = sb("qk_st", [P, 2, 2, J, G * N], f32r)
        v_sb = sb("v_sb", [P, 4, C, D])
        probs = sb("probs", [P, 4, C, N])
        nmax = sb("nmax", [P, 2, H, C])
        zsum = sb("zsum", [P, 2, H, C])
        zinv = sb("zinv", [P, C, H])
        zrep = sb("zrep", [P, C, H, HD])
        probs_t = sb("probs_t", [P, H, C, N])
        zt = sb("zt", [P, G, N])
        attn = sb("attn", [P, G, N])
        attn_s = sb("attn_s", [P, 2, G, N], f32r)
        x2 = sb("x2", [P, 2, C, D])

        s_ps = [ctx.enter_context(nc.psum_tensor(f"s_ps{n}", [P, C, N], f32)) for n in range(S_BANKS)]
        pt_ps = [ctx.enter_context(nc.psum_tensor(f"pt_ps{n}", [P, C, N], f32)) for n in range(2)]
        o_ps = ctx.enter_context(nc.psum_tensor("o_ps", [P, G, N], f32))
        d_ps = [ctx.enter_context(nc.psum_tensor(f"d_ps{n}", [P, 2, N], f32)) for n in range(2)]

        wait_carrier = sem("wait_carrier")
        adj_in, w0_in, b0_in, qk_w_in, vo_w_in, bv_in, bias_in = map(
            sem, ("adj_in", "w0_in", "b0_in", "qk_w_in", "vo_w_in", "bv_in", "bias_in"))
        ident_zero, ident_ready = sem("ident_zero"), sem("ident_ready")
        adjt_mm, adjt_full, adjt_hi, adjt_ready = map(sem, ("adjt_mm", "adjt_full", "adjt_hi", "adjt_ready"))
        bqs_ready, w0_hi, w0_ready = map(sem, ("bqs_ready", "w0_hi", "w0_ready"))
        far_step, far_ready = sem("far_step"), sem("far_ready")
        wp_ready, w_hi, w_ready, c_mm, c_ready = map(sem, ("wp_ready", "w_hi", "w_ready", "c_mm", "c_ready"))
        x_in = [sem(f"x_in{n}") for n in range(4)]
        st_done = [sem("st0_done"), sem("st1_done")]
        mv_done = [sem("mv0_done"), sem("mv1_done")]
        ve_done = [sem("ve0_done"), sem("ve1_done")]
        rs_done = [sem("rs0_done"), sem("rs1_done")]
        nb_done = [sem("nb0_done"), sem("nb1_done")]
        xb_ready, h0_f, h0_hi, h0_lo = map(sem, ("xb_ready", "h0_f", "h0_hi", "h0_lo"))
        yt_mm, yt_f, yt_hi, yt_lo = map(sem, ("yt_mm", "yt_f", "yt_hi", "yt_lo"))
        out0_mm, x1_ready = sem("out0_mm"), sem("x1_ready")
        h1_ready, x1c_ready = sem("h1_ready"), sem("x1c_ready")
        h1t_mm, h1t_f, h1t_hi, h1t_lo = map(sem, ("h1t_mm", "h1t_f", "h1t_hi", "h1t_lo"))
        qk_proj = [sem("q_proj"), sem("k_proj")]
        qk_full = [sem("q_full"), sem("k_full")]
        qk_hi = [sem("q_hi"), sem("k_hi")]
        qk_lo = [sem("q_lo"), sem("k_lo")]
        v_mm, v_ready = sem("v_mm"), sem("v_ready")
        stacked = [[sem(f"stacked{p}_{j}") for j in range(J)] for p in range(2)]
        qk_mm, min_ready, exp_ready, pt_mm = map(sem, ("qk_mm", "min_ready", "exp_ready", "pt_mm"))
        pt_out = [sem("pt_out0"), sem("pt_out1")]
        pv_mm, zinv_ready, zrep_ready, zt_mm, zt_ready = map(
            sem, ("pv_mm", "zinv_ready", "zrep_ready", "zt_mm", "zt_ready"))
        attn_f, attn_hi, attn_lo = sem("attn_f"), sem("attn_hi"), sem("attn_lo")
        out1_mm, x2_ready = sem("out1_mm"), sem("x2_ready")
        stored = [sem("stored0"), sem("stored1")]

        rows = lambda ap: ap.rearrange("(p c) d -> p c d", c=C)
        feat = lambda ap: ap.rearrange("(k p) n -> p k n", p=P)
        BIAS_LOADS = 1 + 2 * J

        LOOP_FROM = 3
        LOOP_STEPS = (LAST - 5 - LOOP_FROM + 1) // UNROLL * UNROLL

        def steps(eng, step):
            for n in range(0, LOOP_FROM):
                step(Batch(0, n), n)
            with eng.Fori(0, LOOP_STEPS // UNROLL) as i:
                for u in range(UNROLL):
                    step(Batch(i, LOOP_FROM + u), None)
            for n in range(LOOP_FROM + LOOP_STEPS, B + 1):
                step(Batch(0, n), n)

        def has(n, d):
            return n is None or 0 <= n + d <= LAST

        def draining(n):
            return n is not None and n >= B - 2

        def ahead(b, h):
            return (b, h, 0) if h < H else (b.plus(1), h - H, 1)

        block = ctx.enter_context(nc.Block())

        @block.sync
        def _(sp):
            def load(dst, src, arrived, short=False):
                sp.dma_start(dst, src, allow_slow_non_contiguous=short).then_inc(arrived, 16)

            def load_x(b):
                sp.dma_start(xt[:, b.slot(4), :, :], rows(x[b.index(), :, :])).then_inc(x_in[b.slot(4)], 16)

            load_x(Batch(0, 0))
            load(w_in[:, 0, :, :], feat(w0), w0_in)
            load(b0_bc[:, :], b0.partition_broadcast(P), b0_in)
            load_x(Batch(0, 1))
            load(w_in[:, 1, :, :], feat(wq), qk_w_in)
            load(w_in[:, 2, :, :], feat(wk), qk_w_in)
            load_x(Batch(0, 2))
            load(w_in[:, 3, :, :], feat(wv), vo_w_in)
            load(w_in[:, 4, :, :], feat(wo), vo_w_in)
            load(bv_col[:, :], bv.rearrange("(k p) -> p k", p=P), bv_in, short=True)
            load(bo_bc[:, :], bo.partition_broadcast(P), bias_in)
            for j in range(J):
                for col, src in ((bq_col, bq), (bk_col, bk)):
                    load(col[HD * j:HD * (j + 1), :],
                         src[2 * HD * j:2 * HD * (j + 1)].rearrange("(g d) -> d g", g=G), bias_in, short=True)

            def store(b):
                wait(sp, x2_ready, b.count(1, 1))
                sp.dma_start(rows(out[b.index(), :, :]), x2[:, b.slot(2), :, :]).then_inc(stored[b.slot(2)], 16)

            def stack(b):
                p = b.slot(2)
                wait(sp, qk_lo[1], b.count(1, 1))
                for j in range(J):
                    for r in range(4):
                        src = qk_s[HD * j:HD * (j + 1), p, :, :, :].rearrange("p t s n -> p (t s) n")
                        q_part, k_part = r % 2, 2 + r // 2
                        sp.dma_start(
                            qk_st[HD * r:HD * (r + 1), p, :, j, :].bitcast(f32),
                            src[:, q_part:k_part + 1:k_part - q_part, :].bitcast(f32),
                        ).then_inc(stacked[p][j], 16)

            def fill():
                load_x(Batch(0, 3))
                sp.wait_ge(h0_lo, 1)
                sp.wait_ge(xb_ready, 1)
                load_x(Batch(0, 4))
                for u in range(2):
                    stack(Batch(0, u))

            def step(b, n):
                if has(n, -2):
                    store(b.plus(-2))
                if has(n, 5):
                    nxt = b.plus(5)
                    wait(sp, h0_lo, nxt.count(1, -3))
                    if n is not None and n <= 2:
                        wait(sp, xb_ready, nxt.count(1, -3))
                    load_x(nxt)
                if has(n, 2):
                    stack(b.plus(2))

            fill()
            steps(sp, step)
            store(Batch(0, LAST))
            sp.wait_ge(stored[0], 16 * (B // 2))
            sp.wait_ge(stored[1], 16 * (B // 2))

        @block.gpsimd
        def _(pool):
            nc.gpsimd.memset(ident[:, :], 0.0).then_inc(ident_zero, 1)
            pool.wait_ge(ident_zero, 1)
            nc.gpsimd.affine_select(out=ident[:, :], in_=ident[:, :], compare_op=ALU.not_equal, fill=1.0,
                                    base=0, pattern=[[-1, P]], channel_multiplier=1).then_inc(ident_ready, 1)
            nc.gpsimd.memset(neghalf[:, :], -0.5)
            nc.gpsimd.memset(minus_one[:, :], -1.0)
            nc.gpsimd.memset(eps[:, :], EPS)
            nc.gpsimd.memset(ones[:, :], 1.0).then_inc(ident_ready, 1)
            pool.wait_ge(ident_ready, 2)

            def rest(dst, full, hi, done):
                nc.gpsimd.tensor_tensor(dst, full, hi.bitcast(f32), ALU.subtract).then_inc(done, 1)

            def factors(b, m, used):
                wait(pool, mv_done[m], b.count(1, 1))
                nc.gpsimd.tensor_tensor(ve[m][:, 1, :], mv[m][:, :, 0], minus_one[:, :], ALU.mult)
                nc.gpsimd.tensor_tensor(ve[m][:, 0, :], mv[m][:, :, 1], eps[:, :], ALU.add).then_inc(
                    ve_done[m], 1)
                wait(pool, used, b.count(1, 0))
                wait(pool, ve_done[m], b.count(1, 1))
                nc.gpsimd.tensor_tensor(rs[m][:, :], ve[m][:, 0, :], neghalf[:, :], ALU.pow).then_inc(
                    rs_done[m], 1)
                wait(pool, rs_done[m], b.count(1, 1))
                nc.gpsimd.tensor_tensor(nb[m][:, :], ve[m][:, 1, :], rs[m][:, :], ALU.mult).then_inc(
                    nb_done[m], 1)

            def add_b0(b):
                wait(pool, x_in[b.slot(4)], b.turn(4, 16, 16))
                wait(pool, x1_ready, b.count(1, -1))
                bc = b0_bc[:, :].unsqueeze(1).broadcast_to([P, C, D])
                nc.gpsimd.tensor_tensor(xb[:, b.slot(2), :, :], xt[:, b.slot(4), :, :], bc,
                                        ALU.add).then_inc(xb_ready, 1)

            def add_c(b):
                wait(pool, x1_ready, b.count(1, 1))
                wait(pool, x2_ready, b.count(1, -3))
                bc = c_bc[:, :].unsqueeze(1).broadcast_to([P, C, D])
                nc.gpsimd.tensor_tensor(x1c[:, b.slot(4), :, :], x1[:, :, :], bc,
                                        ALU.add).then_inc(x1c_ready, 1)

            def replicate_sums(b):
                wait(pool, zinv_ready, b.count(1, 1))
                wait(pool, zt_mm, b.count(1, 0))
                nc.gpsimd.tensor_tensor(
                    zrep[:, :, :, :].rearrange("p c h d -> p (c h) d"),
                    zinv[:, :, :].rearrange("p c h -> p (c h)").unsqueeze(2).broadcast_to([P, C * H, HD]),
                    ones[:, :].unsqueeze(1).broadcast_to([P, C * H, HD]), ALU.mult).then_inc(zrep_ready, 1)

            def low_part(b, parts, full, hi_ready, used, done):
                wait(pool, hi_ready, b.count(1, 1))
                wait(pool, used, b.count(1, 0))
                rest(parts[:, LO], full[:, :, :], parts[:, HI], done)

            def qk_low_part(b, t):
                wait(pool, qk_hi[t], b.count(1, 1))
                r = b.slot(2)
                rest(qk_s[:, r, t, LO, :], qk_f[:, t, :], qk_s[:, r, t, HI, :], qk_lo[t])

            def weight_low_part(m):
                pool.wait_ge(w_hi, m + 1)
                parts, full = ((wq_s, wp[:, 0].rearrange("p k g n -> p k (g n)")),
                               (wk_s, wp[:, 1].rearrange("p k g n -> p k (g n)")),
                               (wv_s, w_in[:, 3]), (wo_s, w_in[:, 4]))[m]
                rest(parts[:, LO], full, parts[:, HI], w_ready)

            def fill():
                first = [Batch(0, u) for u in range(4)]
                factors(first[0], 0, h0_f)
                pool.wait_ge(b0_in, 16)
                add_b0(first[0])
                factors(first[1], 0, h0_f)
                add_b0(first[1])
                factors(first[2], 0, h0_f)
                weight_low_part(0)
                weight_low_part(1)
                factors(first[0], 1, h1_ready)
                pool.wait_ge(c_ready, 1)
                add_c(first[0])
                weight_low_part(2)
                add_b0(first[2])
                weight_low_part(3)
                factors(first[1], 1, h1_ready)
                add_c(first[1])
                factors(first[3], 0, h0_f)
                factors(first[2], 1, h1_ready)
                add_b0(first[3])

            def step(b, n):
                if has(n, -1):
                    replicate_sums(b.plus(-1))
                if has(n, 2):
                    add_c(b.plus(2))
                    low_part(b.plus(2), h1t_s, h1t, h1t_hi, v_mm, h1t_lo)
                if has(n, 3):
                    low_part(b.plus(3), yt_s, yt, yt_hi, out0_mm, yt_lo)
                if has(n, 4):
                    factors(b.plus(4), 0, h0_f)
                    add_b0(b.plus(4))
                if has(n, -1) and n != B:
                    low_part(b.plus(-1), attn_s, attn, attn_hi, out1_mm, attn_lo)
                if has(n, 2):
                    qk_low_part(b.plus(2), 0)
                if has(n, 3):
                    factors(b.plus(3), 1, h1_ready)
                if has(n, 4):
                    low_part(b.plus(4), h0_s, h0, h0_hi, yt_mm, h0_lo)
                if has(n, 2):
                    qk_low_part(b.plus(2), 1)

            fill()
            steps(pool, step)

        @block.vector
        def _(dve):
            def split_constant(parts, full, hi_done, done):
                nc.vector.tensor_copy(parts[:, HI], full).then_inc(hi_done, 1)
                dve.wait_ge(hi_done, 1)
                nc.vector.tensor_tensor(parts[:, LO], full, parts[:, HI].bitcast(f32),
                                        ALU.subtract).then_inc(done, 1)

            def setup_adj():
                dve.wait_ge(adjt_mm, 1)
                nc.vector.tensor_copy(adj_f[:, :, :], pt_ps[0][:, :, :]).then_inc(adjt_full, 1)
                dve.wait_ge(adjt_full, 1)
                split_constant(adj_t, adj_f[:, :, :], adjt_hi, adjt_ready)

            def setup_w0():
                dve.wait_ge(w0_in, 16)
                split_constant(w0_s, w_in[:, 0], w0_hi, w0_ready)

            def setup_biases():
                dve.wait_ge(bias_in, 16 * BIAS_LOADS)
                nc.vector.tensor_scalar(bqs[:, :], bq_col[:, :], SCALE, None, ALU.mult).then_inc(bqs_ready, 1)
                dve.wait_ge(c_mm, 1)
                nc.vector.tensor_tensor(c_bc[:, :], pt_ps[1][:, 0, :], bo_bc[:, :], ALU.add).then_inc(c_ready, 1)

            def setup_far():
                by_chunk = adj_nat[:, :, :].rearrange("p c (k d) -> p c d k", d=C)
                for c in range(C):
                    nc.vector.tensor_scalar(far[:, c, :].rearrange("p (d k) -> p d k", d=C),
                                            by_chunk[:, c, :, :], -1.0, 1.0, ALU.mult,
                                            ALU.add).then_inc(far_step, 1)
                dve.wait_ge(far_step, C)
                nc.vector.tensor_scalar(far[:, :, :], far[:, :, :], FAR, None, ALU.mult).then_inc(far_ready, 1)
                dve.wait_ge(far_ready, 1)

            def high_part(b, parts, full, f_ready, used, done):
                wait(dve, f_ready, b.count(1, 1))
                wait(dve, used, b.count(1, 0))
                nc.vector.tensor_copy(parts[:, HI], full[:, :, :]).then_inc(done, 1)

            def split(b, parts, full, f_ready, used, hi_ready, lo_ready):
                high_part(b, parts, full, f_ready, used, hi_ready)
                wait(dve, hi_ready, b.count(1, 1))
                nc.vector.tensor_tensor(parts[:, LO], full[:, :, :], parts[:, HI].bitcast(f32),
                                        ALU.subtract).then_inc(lo_ready, 1)

            def qk_high_part(b, t):
                r = b.slot(2)
                wait(dve, qk_full[t], b.count(1, 1))
                for j in range(J):
                    wait(dve, stacked[r][j], b.turn(2, 64, 0))
                nc.vector.tensor_copy(qk_s[:, r, t, HI, :], qk_f[:, t, :]).then_inc(qk_hi[t], 1)

            def qk_split(b, t):
                qk_high_part(b, t)
                r = b.slot(2)
                wait(dve, qk_hi[t], b.count(1, 1))
                nc.vector.tensor_tensor(qk_s[:, r, t, LO, :], qk_f[:, t, :], qk_s[:, r, t, HI, :].bitcast(f32),
                                        ALU.subtract).then_inc(qk_lo[t], 1)

            def stats(b, src, m):
                for c in range(C):
                    last = nc.vector.bn_stats(st[m][:, c, :], src[:, c, :])
                last.then_inc(st_done[m], 1)
                wait(dve, st_done[m], b.count(1, 1))
                wait(dve, nb_done[m], b.count(1, 0))
                dve.sem_inc(wait_carrier)
                for c in range(C):
                    last = nc.vector.bn_aggr(mv[m][:, c, :], st[m][:, c, :])
                last.then_inc(mv_done[m], 1)

            def stats_x(b):
                wait(dve, x_in[b.slot(4)], b.turn(4, 16, 16))
                stats(b, xt[:, b.slot(4), :, :], 0)

            def graph_residual(b):
                wait(dve, out0_mm, b.count(1, 1))
                wait(dve, xb_ready, b.count(1, 1))
                wait(dve, x1c_ready, b.count(1, 0))
                wait(dve, h1_ready, b.count(1, 0))
                nc.vector.tensor_tensor(x1[:, :, :], d_ps[0][:, :, :], xb[:, b.slot(2), :, :],
                                        ALU.add).then_inc(x1_ready, 1)

            def stats_x1(b):
                wait(dve, x1_ready, b.count(1, 1))
                dve.sem_inc(wait_carrier)
                stats(b, x1, 1)

            def attention_residual(b):
                wait(dve, out1_mm, b.count(1, 1))
                wait(dve, x1c_ready, b.count(1, 1))
                wait(dve, stored[b.slot(2)], b.turn(2, 16, 0))
                nc.vector.tensor_tensor(x2[:, b.slot(2), :, :], d_ps[1][:, :, :],
                                        x1c[:, b.slot(4), :, :], ALU.add).then_inc(x2_ready, 1)

            def find_min(b, n, h):
                b, h, d = ahead(b, h)
                if has(n, d):
                    wait(dve, qk_mm, b.count(H, h + 1))
                    dve.sem_inc(wait_carrier)
                    bank = s_ps[h % S_BANKS]
                    for c in range(C):
                        last = nc.vector.tensor_tensor_reduce(
                            bank[:, c, :], bank[:, c, :], far[:, c, :], 1.0, BIG, ALU.add, ALU.min,
                            nmax[:, b.slot(2), h, c:c + 1])
                    last.then_inc(min_ready, 1)

            def move_probs(b, h):
                wait(dve, pt_mm, b.count(H, h + 1))
                wait(dve, pv_mm, b.count(G, h // HG + 1 - G))
                nc.vector.tensor_copy(probs_t[:, h, :, :], pt_ps[h % 2][:, :, :]).then_inc(pt_out[h % 2], 1)

            def invert_sums(b):
                wait(dve, exp_ready, b.count(H, H))
                wait(dve, zrep_ready, b.count(1, 0))
                nc.vector.reciprocal(zinv[:, :, :],
                                     zsum[:, b.slot(2), :, :].rearrange("p h c -> p c h")).then_inc(zinv_ready, 1)

            def normalise(b):
                wait(dve, zt_ready, b.count(1, 1))
                wait(dve, pv_mm, b.count(G, G))
                wait(dve, attn_lo, b.count(1, 0))
                nc.vector.tensor_tensor(attn[:, :, :], o_ps[:, :, :], zt[:, :, :], ALU.mult).then_inc(attn_f, 1)

            def fill():
                first = [Batch(0, u) for u in range(4)]
                stats_x(first[0])
                setup_adj()
                split(first[0], h0_s, h0, h0_f, yt_mm, h0_hi, h0_lo)
                stats_x(first[1])
                setup_w0()
                stats_x(first[2])
                split(first[0], yt_s, yt, yt_f, out0_mm, yt_hi, yt_lo)
                split(first[1], h0_s, h0, h0_f, yt_mm, h0_hi, h0_lo)
                setup_biases()
                graph_residual(first[0])
                stats_x1(first[0])
                split(first[1], yt_s, yt, yt_f, out0_mm, yt_hi, yt_lo)
                split(first[2], h0_s, h0, h0_f, yt_mm, h0_hi, h0_lo)
                graph_residual(first[1])
                split(first[0], h1t_s, h1t, h1t_f, v_mm, h1t_hi, h1t_lo)
                stats_x1(first[1])
                split(first[2], yt_s, yt, yt_f, out0_mm, yt_hi, yt_lo)
                qk_split(first[0], 0)
                qk_split(first[0], 1)
                stats_x(first[3])
                graph_residual(first[2])
                split(first[1], h1t_s, h1t, h1t_f, v_mm, h1t_hi, h1t_lo)
                stats_x1(first[2])
                split(first[3], h0_s, h0, h0_f, yt_mm, h0_hi, h0_lo)
                setup_far()
                find_min(first[0], 0, 0)
                qk_split(first[1], 0)
                find_min(first[0], 0, 1)
                qk_split(first[1], 1)

            def step(b, n):
                for h in range(H):
                    if h in (2, 4) and has(n, 0):
                        move_probs(b, h - 1)
                    if h == 4 and draining(n):
                        normalise(b.plus(-1))
                    find_min(b, n, h + 2)
                    if h == 0 and draining(n):
                        attention_residual(b.plus(-2))
                    if h == 1 and has(n, 2):
                        high_part(b.plus(2), h1t_s, h1t, h1t_f, v_mm, h1t_hi)
                    if h == 2 and has(n, 3):
                        high_part(b.plus(3), yt_s, yt, yt_f, out0_mm, yt_hi)
                    if h == 2 and has(n, 4):
                        stats_x(b.plus(4))
                    if h == 4 and has(n, -1):
                        if not draining(n):
                            normalise(b.plus(-1))
                        if n == B:
                            split(b.plus(-1), attn_s, attn, attn_f, out1_mm, attn_hi, attn_lo)
                        else:
                            high_part(b.plus(-1), attn_s, attn, attn_f, out1_mm, attn_hi)
                    if h == 5 and has(n, 2):
                        qk_high_part(b.plus(2), 0)
                    if h == 5 and has(n, 3):
                        graph_residual(b.plus(3))
                        stats_x1(b.plus(3))
                    if h == 6 and has(n, 0):
                        move_probs(b, 6)
                    if h == 6 and has(n, 4):
                        high_part(b.plus(4), h0_s, h0, h0_f, yt_mm, h0_hi)
                    if h == 7 and has(n, 2):
                        qk_high_part(b.plus(2), 1)
                    if h == 7 and has(n, 0):
                        invert_sums(b)
                        move_probs(b, 7)
                    if h == 7 and has(n, -1) and (n is None or n < B - 3 or n == B):
                        attention_residual(b.plus(-1))

            fill()
            steps(dve, step)

        @block.scalar
        def _(act):
            nc.scalar.dma_start(adj_nat[:, :, :], rows(adj)).then_inc(adj_in, 16)

            def prepare_qk_weights():
                act.wait_ge(qk_w_in, 32)
                for k in range(K):
                    for m, s in ((0, SCALE), (1, 1.0)):
                        last = nc.scalar.activation(
                            wp[:, m, k, :, :].rearrange("p g (j d) -> p g j d", j=J),
                            w_in[:, 1 + m, k, :].rearrange("p (j g d) -> p g j d", j=J, g=G), ACT.Copy, scale=s)
                last.then_inc(wp_ready, 1)
                act.wait_ge(wp_ready, 1)
                for m, parts in enumerate((wq_s, wk_s)):
                    nc.scalar.activation(parts[:, HI], wp[:, m].rearrange("p k g n -> p k (g n)"),
                                         ACT.Copy).then_inc(w_hi, 1)

            def prepare_vo_weights():
                act.wait_ge(vo_w_in, 32)
                for m, parts in enumerate((wv_s, wo_s)):
                    nc.scalar.activation(parts[:, HI], w_in[:, 3 + m], ACT.Copy).then_inc(w_hi, 1)

            def normed(b, dst, src, m, used, ready):
                wait(act, nb_done[m], b.count(1, 1))
                wait(act, used, b.count(1, 0))
                for c in range(C):
                    last = nc.scalar.activation(dst[:, c, :], src[:, c, :], ACT.Relu, bias=nb[m][:, c:c + 1],
                                                scale=rs[m][:, c:c + 1])
                last.then_inc(ready, 1)

            def norm_x(b):
                normed(b, h0, xt[:, b.slot(4), :, :], 0, h0_lo, h0_f)

            def norm_x1(b):
                normed(b, h1, x1, 1, h1t_mm, h1_ready)

            def move(b, dst, bank, filled, used, ready, ring=1):
                wait(act, filled, b.count(1, 1))
                wait(act, used, b.count(1, 1 - ring))
                nc.scalar.activation(dst, bank[:, :, :], ACT.Copy).then_inc(ready, 1)

            def move_yt(b, bank=1):
                move(b, yt[:, :, :], d_ps[bank], yt_mm, yt_lo, yt_f)

            def move_h1t(b, bank=0):
                move(b, h1t[:, :, :], d_ps[bank], h1t_mm, h1t_lo, h1t_f)

            def move_v(b, bank=0):
                move(b, v_sb[:, b.slot(4), :, :], d_ps[bank], v_mm, x2_ready, v_ready, ring=4)

            def qk_move(b, t, col, bank=1):
                wait(act, qk_proj[t], b.count(1, 1))
                wait(act, qk_lo[t], b.count(1, 0))
                for g in range(G):
                    last = nc.scalar.activation(qk_f[:, t, N * g:N * (g + 1)], d_ps[bank][:, g, :], ACT.Identity,
                                                bias=col[:, g:g + 1])
                last.then_inc(qk_full[t], 1)

            def exponentials(b, n, h):
                b, h, d = ahead(b, h)
                if has(n, d):
                    wait(act, min_ready, b.count(H, h + 1))
                    wait(act, pt_mm, b.count(H, h + 1 - 4))
                    if h == 0:
                        wait(act, zinv_ready, b.count(1, -1))
                    for c in range(C):
                        last = nc.scalar.activation(
                            probs[:, h % 4, c, :], s_ps[h % S_BANKS][:, c, :], ACT.Exp,
                            bias=nmax[:, b.slot(2), h, c:c + 1], scale=-1.0,
                            accum_out=zsum[:, b.slot(2), h, c:c + 1])
                    last.then_inc(exp_ready, 1)

            def move_probs(b, h):
                wait(act, pt_mm, b.count(H, h + 1))
                wait(act, pv_mm, b.count(G, h // HG + 1 - G))
                nc.scalar.activation(probs_t[:, h, :, :], pt_ps[h % 2][:, :, :], ACT.Copy).then_inc(
                    pt_out[h % 2], 1)

            def fill():
                first = [Batch(0, u) for u in range(4)]
                norm_x(first[0])
                prepare_qk_weights()
                move_yt(first[0], 1)
                norm_x(first[1])
                prepare_vo_weights()
                move_yt(first[1], 1)
                norm_x(first[2])
                norm_x1(first[0])
                move_h1t(first[0], 1)
                move_yt(first[2], 0)
                act.wait_ge(bqs_ready, 1)
                qk_move(first[0], 0, bqs, 1)
                qk_move(first[0], 1, bk_col, 0)
                norm_x1(first[1])
                move_v(first[0], 1)
                move_h1t(first[1], 1)
                norm_x(first[3])
                qk_move(first[1], 0, bqs, 0)
                norm_x1(first[2])
                qk_move(first[1], 1, bk_col, 1)
                exponentials(first[0], 0, 0)
                move_v(first[1], 0)

            def step(b, n):
                for h in range(H):
                    if h == 2 and has(n, 3):
                        move_yt(b.plus(3))
                    exponentials(b, n, h + 1)
                    if h in (3, 5) and has(n, 0):
                        move_probs(b, h - 1)
                    if h == 7 and has(n, 2):
                        move_v(b.plus(2))
                    if h == 0 and has(n, 0):
                        move_probs(b, 0)
                    if h == 0 and has(n, 2):
                        move_h1t(b.plus(2))
                    if h == 3 and has(n, -1):
                        move(b.plus(-1), zt[:, :, :], d_ps[0], zt_mm, attn_f, zt_ready)
                    if h == 4 and has(n, 2):
                        qk_move(b.plus(2), 0, bqs)
                    if h == 5 and has(n, 4):
                        norm_x(b.plus(4))
                    if h == 6 and has(n, 2):
                        qk_move(b.plus(2), 1, bk_col)
                    if h == 6 and has(n, 0):
                        move_probs(b, 5)
                    if h == 7 and has(n, 3):
                        norm_x1(b.plus(3))

            fill()
            steps(act, step)

        @block.tensor
        def _(pe):
            def transpose_adj():
                pe.wait_ge(ident_ready, 1)
                pe.wait_ge(adj_in, 16)
                for d in range(C):
                    for c in range(C):
                        last = nc.tensor.transpose(pt_ps[0][:, d, P * c:P * (c + 1)], adj_nat[:, c, d::C],
                                                   ident[:, :])
                last.then_inc(adjt_mm, 1)

            def bias_product():
                pe.wait_ge(vo_w_in, 32)
                pe.wait_ge(bv_in, 16)
                for k in range(K):
                    last = nc.tensor.matmul(pt_ps[1][:, 0, :], bv_col[:, k:k + 1].broadcast_to([P, P]),
                                            w_in[:, 4, k, :], start=(k == 0), stop=(k == K - 1))
                last.then_inc(c_mm, 1)

            def product(dst, left, right, chunks):
                passes = [(k, a, b) for a, b in ((LO, HI), (HI, LO), (HI, HI)) for k in range(chunks)]
                for m, (k, a, b) in enumerate(passes):
                    last = nc.tensor.matmul(dst, left(a, k), right(b, k), start=(m == 0),
                                            stop=(m == len(passes) - 1))
                return last

            def aggregate(b, bank=1):
                wait(pe, h0_hi, b.count(1, 1))
                wait(pe, h0_lo, b.count(1, 1))
                for k in range(K):
                    last = product(d_ps[bank][:, k, :], lambda s, c: h0_s[:, s, c, P * k:P * (k + 1)],
                                   lambda s, c: adj_t[:, s, c, :], C)
                last.then_inc(yt_mm, 1)

            def graph_product(b, bank=0):
                wait(pe, yt_hi, b.count(1, 1))
                wait(pe, yt_lo, b.count(1, 1))
                for c in range(C):
                    last = product(d_ps[bank][:, c, :], lambda s, k: yt_s[:, s, k, P * c:P * (c + 1)],
                                   lambda s, k: w0_s[:, s, k, :], K)
                last.then_inc(out0_mm, 1)

            def transpose_h1(b, bank=0):
                wait(pe, h1_ready, b.count(1, 1))
                for k in range(K):
                    for c in range(C):
                        last = nc.tensor.transpose(d_ps[bank][:, k, P * c:P * (c + 1)],
                                                   h1[:, c, P * k:P * (k + 1)], ident[:, :])
                last.then_inc(h1t_mm, 1)

            def project_qk(b, t, w, bank=1):
                wait(pe, h1t_hi, b.count(1, 1))
                wait(pe, h1t_lo, b.count(1, 1))
                for g in range(G):
                    last = product(d_ps[bank][:, g, :], lambda s, k: w[:, s, k, P * g:P * (g + 1)],
                                   lambda s, k: h1t_s[:, s, k, :], K)
                last.then_inc(qk_proj[t], 1)

            def project_v(b, bank=0):
                for c in range(C):
                    last = product(d_ps[bank][:, c, :], lambda s, k: h1t_s[:, s, k, P * c:P * (c + 1)],
                                   lambda s, k: wv_s[:, s, k, :], K)
                last.then_inc(v_mm, 1)

            def scores(b, n, h):
                b, h, d = ahead(b, h)
                if has(n, d):
                    if h % 2 == 0:
                        wait(pe, stacked[b.slot(2)][h // 2], b.turn(2, 64, 64))
                    wait(pe, exp_ready, b.count(H, h - 2 if h >= S_BANKS else (-1, 0, -2)[h]))
                    for c in range(C):
                        last = nc.tensor.matmul(
                            s_ps[h % S_BANKS][:, c, :],
                            qk_st[:, b.slot(2), 0, h // 2, N * (h % 2) + P * c:N * (h % 2) + P * (c + 1)],
                            qk_st[:, b.slot(2), 1, h // 2, N * (h % 2):N * (h % 2 + 1)],
                            start=True, stop=True)
                    last.then_inc(qk_mm, 1)

            def transpose_probs(b, h):
                wait(pe, exp_ready, b.count(H, h + 1))
                wait(pe, pt_out[h % 2], b.count(HG, h // 2))
                for d in range(C):
                    for c in range(C):
                        last = nc.tensor.transpose(pt_ps[h % 2][:, d, P * c:P * (c + 1)],
                                                   probs[:, h % 4, c, P * d:P * (d + 1)], ident[:, :])
                last.then_inc(pt_mm, 1)

            def transpose_sums(b):
                wait(pe, zrep_ready, b.count(1, 1))
                for g in range(G):
                    for c in range(C):
                        last = nc.tensor.transpose(
                            d_ps[0][:, g, P * c:P * (c + 1)],
                            zrep[:, c, HG * g:HG * (g + 1), :].rearrange("p h d -> p (h d)"), ident[:, :])
                last.then_inc(zt_mm, 1)

            def weighted(b, g):
                wait(pe, v_ready, b.count(1, 1))
                for half in range(2):
                    wait(pe, pt_out[half], b.count(HG, 2 * (g + 1)))
                if g == 0:
                    wait(pe, attn_f, b.count(1, 0))
                for c in range(C):
                    for j in range(HG):
                        h = HG * g + j
                        last = nc.tensor.matmul(o_ps[HD * j:HD * (j + 1), g, :],
                                                v_sb[:, b.slot(4), c, HD * h:HD * (h + 1)],
                                                probs_t[:, h, c, :], start=(c == 0), stop=(c == C - 1))
                last.then_inc(pv_mm, 1)

            def output_product(b):
                wait(pe, attn_hi, b.count(1, 1))
                wait(pe, attn_lo, b.count(1, 1))
                for c in range(C):
                    last = product(d_ps[1][:, c, :], lambda s, g: attn_s[:, s, g, P * c:P * (c + 1)],
                                   lambda s, g: wo_s[:, s, g, :], G)
                last.then_inc(out1_mm, 1)

            def fill():
                first = [Batch(0, u) for u in range(3)]
                transpose_adj()
                pe.wait_ge(adjt_ready, 1)
                aggregate(first[0], 1)
                bias_product()
                pe.wait_ge(w0_ready, 1)
                graph_product(first[0], 0)
                pe.wait_ge(yt_f, 1)
                aggregate(first[1], 1)
                pe.wait_ge(x1_ready, 1)
                graph_product(first[1], 0)
                pe.wait_ge(yt_f, 2)
                transpose_h1(first[0], 1)
                pe.wait_ge(x1_ready, 2)
                aggregate(first[2], 0)
                pe.wait_ge(h1t_f, 1)
                pe.wait_ge(w_ready, 1)
                project_qk(first[0], 0, wq_s, 1)
                pe.wait_ge(yt_f, 3)
                pe.wait_ge(w_ready, 2)
                project_qk(first[0], 1, wk_s, 0)
                pe.wait_ge(qk_full[0], 1)
                pe.wait_ge(w_ready, 4)
                project_v(first[0], 1)
                pe.wait_ge(qk_full[1], 1)
                graph_product(first[2], 0)
                pe.wait_ge(v_ready, 1)
                transpose_h1(first[1], 1)
                pe.wait_ge(x1_ready, 3)
                project_qk(first[1], 0, wq_s, 0)
                scores(first[0], 0, 0)
                pe.wait_ge(h1t_f, 2)
                project_qk(first[1], 1, wk_s, 1)
                scores(first[0], 0, 1)
                pe.wait_ge(qk_full[0], 2)
                project_v(first[1], 0)

            def step(b, n):
                for h in range(H):
                    if not (draining(n) and h in (0, 3)):
                        scores(b, n, h + 2)
                    if has(n, 0):
                        transpose_probs(b, h)
                    if draining(n) and h == 2:
                        scores(b, n, 5)
                    if n is not None and draining(n + 1) and h == 7:
                        scores(b, n, H + 2)
                    if h == 0 and has(n, 2):
                        wait(pe, v_ready, b.count(1, 2))
                        transpose_h1(b.plus(2))
                    if h == 1 and has(n, 3):
                        if has(n, -2):
                            wait(pe, x2_ready, b.count(1, -1))
                        else:
                            wait(pe, qk_full[1], b.count(1, 2))
                        aggregate(b.plus(3))
                    if h == 2 and has(n, -1):
                        if has(n, 2):
                            wait(pe, h1t_f, b.count(1, 3))
                        elif has(n, 1):
                            wait(pe, v_ready, b.count(1, 2))
                        else:
                            wait(pe, zt_ready, b.count(1, -1))
                        transpose_sums(b.plus(-1))
                        weighted(b.plus(-1), 1)
                    if h == 3 and has(n, 2):
                        if has(n, 3):
                            wait(pe, yt_f, b.count(1, 4))
                        else:
                            wait(pe, x2_ready, b.count(1, -1))
                        project_qk(b.plus(2), 0, wq_s)
                    if h == 4 and has(n, 3):
                        if has(n, -1):
                            wait(pe, zt_ready, b.count(1, 0))
                        else:
                            wait(pe, h1t_f, b.count(1, 3))
                        graph_product(b.plus(3))
                    if h == 5 and has(n, 2):
                        wait(pe, qk_full[0], b.count(1, 3))
                        project_qk(b.plus(2), 1, wk_s)
                    if h == 5 and has(n, 0):
                        weighted(b, 0)
                    if h == 6 and has(n, 2):
                        if has(n, 3):
                            wait(pe, x1_ready, b.count(1, 4))
                        else:
                            wait(pe, zt_ready, b.count(1, 0))
                        project_v(b.plus(2))
                    if h == 7 and has(n, -1):
                        if has(n, 2):
                            wait(pe, qk_full[1], b.count(1, 3))
                        else:
                            wait(pe, x2_ready, b.count(1, -1))
                        output_product(b.plus(-1))

            fill()
            steps(pe, step)


_INS = ['x', 'adj', 'L0_gnn_weight', 'L0_gnn_bias', 'L1_gnn_Wq', 'L1_gnn_bq', 'L1_gnn_Wk', 'L1_gnn_bk',
        'L1_gnn_Wv', 'L1_gnn_bv', 'L1_gnn_Wo', 'L1_gnn_bo']


def kernel(**inputs):
    import numpy as _np
    import concourse.bacc as _bacc
    from concourse import mybir as _mybir
    from concourse.bass_utils import run_bass_kernel_spmd as _run

    nc = _bacc.Bacc("TRN2", target_bir_lowering=False, num_devices=1)
    arrays, args = {}, []
    for name in _INS:
        a = _np.ascontiguousarray(inputs[name])
        arrays[f"in_{name}_dram"] = a
        args.append(nc.dram_tensor(f"in_{name}_dram", a.shape, _mybir.dt.from_np(a.dtype), kind="ExternalInput").ap())
    args.append(nc.dram_tensor("out_0_dram", inputs["x"].shape, _mybir.dt.float32, kind="ExternalOutput").ap())
    gnn_attention_kernel(nc, *args)
    r = _run(nc, [arrays], core_ids=[0])
    return r.results[0]["out_0_dram"]
```
